# Optimizing a Trainium2 kernel written in Bass

```python
import numpy as np
import jax
import jax.numpy as jnp

def _softmax(x, axis=-1):
    return jax.nn.softmax(x, axis=axis)

def _gelu(x):
    return jax.nn.gelu(x, approximate=True)

def _silu(x):
    return jax.nn.silu(x)

def _sigmoid(x):
    return jax.nn.sigmoid(x)

def _layernorm(x, axis=-1, eps=1e-05):
    m = jnp.mean(x, axis=axis, keepdims=True)
    v = jnp.var(x, axis=axis, keepdims=True)
    return (x - m) / jnp.sqrt(v + eps)

def _scatter_add(tgt, idx, src, axis=0):
    return tgt.at[idx].add(src)

def _segment_sum(src, seg, n):
    return jax.ops.segment_sum(src, seg, n)
kernel_name = 'mk_flamingo_gated_d1_seqx_r4_06a477'

def setup_inputs(seed: int=0):
    np.random.seed(seed)
    _w = jnp.asarray

    def _rec_inputs():
        import jax
        import jax.numpy as jnp
        _rk = jax.random.key(seed)
        x = 0.5 + 0.2887 * jax.random.normal(jax.random.fold_in(_rk, 1), (4, 512, 512), jnp.float32)
        _lenS = 512 - jax.random.randint(jax.random.fold_in(_rk, 7), (4,), 0, max(1, 512 // 4) + 1, jnp.int32)
        _lenS2 = 512 - jax.random.randint(jax.random.fold_in(_rk, 8), (4,), 0, max(1, 512 // 4) + 1, jnp.int32)
        _ctx_512P = jax.random.normal(jax.random.fold_in(_rk, 11), (4, 16, 128), jnp.float32)
        _ctx_512c = jax.random.dirichlet(jax.random.fold_in(_rk, 511), 0.3 * jnp.ones((16,), jnp.float32), (4, 512))
        _ctx_512t = jnp.einsum('bsk,bkd->bsd', _ctx_512c, _ctx_512P)
        _ctx_512t = _ctx_512t * jax.lax.rsqrt(jnp.mean(jnp.square(_ctx_512t)) + 1e-12) * 0.953939
        ctx_512 = 7.22013e-05 + 1.00017 * (_ctx_512t + 0.3 * jax.random.normal(jax.random.fold_in(_rk, 611), (4, 512, 128), jnp.float32))
        _g = jax.random.normal(jax.random.fold_in(_rk, 9001), (2, 1), jnp.float32)
        _g = jnp.sign(_g) * jnp.maximum(jnp.abs(_g), 1.0) + (_g == 0) * 1.0
        g_xattn = _g[0]
        g_ffn = _g[1]
        return (x, ctx_512, g_xattn, g_ffn)
    x, ctx_512, g_xattn, g_ffn = _rec_inputs()

    def _L0_xattn_setup():
        import jax, jax.numpy as jnp
        import numpy as np
        P_ASEM = 0.6
        key = jax.random.key(seed)
        k1, k2, k3 = jax.random.split(key, 3)
        B, N, D = (8, 512, 128)
        x = jax.random.normal(k1, (B, N, D), dtype=jnp.float32)
        adj = jax.random.uniform(k2, (B, N, N), dtype=jnp.float32)
        bound = 1.0 / np.sqrt(2 * D)
        W = jax.random.uniform(k3, (1, 2 * D), dtype=jnp.float32, minval=-bound, maxval=bound)
        b = jnp.zeros((1,), dtype=jnp.float32)
        return {'x': x, 'adj': adj, 'W': W, 'b': b}
    _L0_xattn_all = _L0_xattn_setup()
    _L0_xattn_in = {k: v for k, v in _L0_xattn_all.items() if k in ('W', 'b')}
    del _L0_xattn_all

    def _L0_ffn_setup():
        import jax, jax.numpy as jnp
        import numpy as np
        NUM_EXPERTS = 32
        TOP_K = 8
        SELECT_TOP_K = 4
        THRESHOLD = 0.5
        HIDDEN = 512
        D_FF = 192

        def _moe_forward(hidden_states, gate_weight, gate_up_proj, down_proj, similarity):
            B, S_len, H = hidden_states.shape
            E, K, Ssel = (NUM_EXPERTS, TOP_K, SELECT_TOP_K)
            x = hidden_states.reshape(-1, H)
            router_logits = x @ gate_weight.T
            router_probs = jax.nn.softmax(router_logits.astype(jnp.float32), axis=-1).astype(router_logits.dtype)
            router_top_value, router_indices = jax.lax.top_k(router_probs, K)
            routing_weights = router_top_value / jnp.clip(jnp.sum(router_top_value, axis=-1, keepdims=True), 1e-12, None)
            sim = similarity.astype(jnp.float32)
            sim = sim.at[jnp.arange(E), jnp.arange(E)].set(1.0)
            prim = router_indices[:, :Ssel]
            sec = router_indices[:, Ssel:]
            sim_cand = sim[sec[:, :, None], prim[:, None, :]]
            best_sim = jnp.max(sim_cand, axis=-1)
            best_i = jnp.argmax(sim_cand, axis=-1)
            prim_rep = jnp.broadcast_to(prim[:, None, :], sim_cand.shape)
            best_primary = jnp.take_along_axis(prim_rep, best_i[..., None], axis=-1)[..., 0]
            new_sec = jnp.where(best_sim < THRESHOLD, sec, best_primary) if THRESHOLD > 0.0 else best_primary
            rerouted_indices = jnp.concatenate([prim, new_sec], axis=1)
            combine = jnp.sum(jax.nn.one_hot(rerouted_indices, E, dtype=routing_weights.dtype) * routing_weights[..., None], axis=1)

            def expert_step(y, params):
                wgu, wd, cw = params
                gu = x @ wgu.T
                g, u = jnp.split(gu, 2, axis=-1)
                h = jax.nn.silu(g) * u
                y = y + h @ wd.T * cw[:, None]
                return (y, None)
            y0 = jnp.zeros_like(x)
            y, _ = jax.lax.scan(expert_step, y0, (gate_up_proj, down_proj, combine.T))
            return y.reshape(B, S_len, H)
        key = jax.random.key(seed)
        ks = jax.random.split(key, 5)
        hidden_states = jax.random.normal(ks[0], (4, 512, HIDDEN), dtype=jnp.float32)
        gate_weight = jax.random.normal(ks[1], (NUM_EXPERTS, HIDDEN), dtype=jnp.float32) * 0.02
        gate_up_proj = jax.random.normal(ks[2], (NUM_EXPERTS, 2 * D_FF, HIDDEN), dtype=jnp.float32) * 0.02
        down_proj = jax.random.normal(ks[3], (NUM_EXPERTS, HIDDEN, D_FF), dtype=jnp.float32) * 0.02
        similarity = jax.random.uniform(ks[4], (NUM_EXPERTS, NUM_EXPERTS), dtype=jnp.float32)
        return {'hidden_states': hidden_states, 'gate_weight': gate_weight, 'gate_up_proj': gate_up_proj, 'down_proj': down_proj, 'similarity': similarity}
    _L0_ffn_all = _L0_ffn_setup()
    _L0_ffn_in = {k: v for k, v in _L0_ffn_all.items() if k in ('gate_weight', 'gate_up_proj', 'down_proj', 'similarity')}
    del _L0_ffn_all
    return {'x': x, 'ctx_512': ctx_512, 'g_xattn': g_xattn, 'g_ffn': g_ffn, 'L0_xattn_W': _L0_xattn_in['W'], 'L0_xattn_b': _L0_xattn_in['b'], 'L0_ffn_gate_weight': _L0_ffn_in['gate_weight'], 'L0_ffn_gate_up_proj': _L0_ffn_in['gate_up_proj'], 'L0_ffn_down_proj': _L0_ffn_in['down_proj'], 'L0_ffn_similarity': _L0_ffn_in['similarity']}

def reference(x, ctx_512, g_xattn, g_ffn, L0_xattn_W, L0_xattn_b, L0_ffn_gate_weight, L0_ffn_gate_up_proj, L0_ffn_down_proj, L0_ffn_similarity):
    import jax
    import jax.numpy as jnp

    def _L0_xattn_ref(x, adj, W, b):
        import jax, jax.numpy as jnp
        import numpy as np
        P_ASEM = 0.6
        D = x.shape[-1]
        Wi = W[:, :D]
        Wj = W[:, D:]
        si = jnp.einsum('bnd,d->bn', x, Wi[0])
        sj = jnp.einsum('bnd,d->bn', x, Wj[0])
        xij = jax.nn.sigmoid(si[:, :, None] + sj[:, None, :] + b[0])
        return P_ASEM * xij + (1.0 - P_ASEM) * adj

    def _L0_ffn_ref(hidden_states, gate_weight, gate_up_proj, down_proj, similarity):
        import jax, jax.numpy as jnp
        import numpy as np
        NUM_EXPERTS = 32
        TOP_K = 8
        SELECT_TOP_K = 4
        THRESHOLD = 0.5
        HIDDEN = 512
        D_FF = 192

        def _moe_forward(hidden_states, gate_weight, gate_up_proj, down_proj, similarity):
            B, S_len, H = hidden_states.shape
            E, K, Ssel = (NUM_EXPERTS, TOP_K, SELECT_TOP_K)
            x = hidden_states.reshape(-1, H)
            router_logits = x @ gate_weight.T
            router_probs = jax.nn.softmax(router_logits.astype(jnp.float32), axis=-1).astype(router_logits.dtype)
            router_top_value, router_indices = jax.lax.top_k(router_probs, K)
            routing_weights = router_top_value / jnp.clip(jnp.sum(router_top_value, axis=-1, keepdims=True), 1e-12, None)
            sim = similarity.astype(jnp.float32)
            sim = sim.at[jnp.arange(E), jnp.arange(E)].set(1.0)
            prim = router_indices[:, :Ssel]
            sec = router_indices[:, Ssel:]
            sim_cand = sim[sec[:, :, None], prim[:, None, :]]
            best_sim = jnp.max(sim_cand, axis=-1)
            best_i = jnp.argmax(sim_cand, axis=-1)
            prim_rep = jnp.broadcast_to(prim[:, None, :], sim_cand.shape)
            best_primary = jnp.take_along_axis(prim_rep, best_i[..., None], axis=-1)[..., 0]
            new_sec = jnp.where(best_sim < THRESHOLD, sec, best_primary) if THRESHOLD > 0.0 else best_primary
            rerouted_indices = jnp.concatenate([prim, new_sec], axis=1)
            combine = jnp.sum(jax.nn.one_hot(rerouted_indices, E, dtype=routing_weights.dtype) * routing_weights[..., None], axis=1)

            def expert_step(y, params):
                wgu, wd, cw = params
                gu = x @ wgu.T
                g, u = jnp.split(gu, 2, axis=-1)
                h = jax.nn.silu(g) * u
                y = y + h @ wd.T * cw[:, None]
                return (y, None)
            y0 = jnp.zeros_like(x)
            y, _ = jax.lax.scan(expert_step, y0, (gate_up_proj, down_proj, combine.T))
            return y.reshape(B, S_len, H)
        return _moe_forward(hidden_states, gate_weight, gate_up_proj, down_proj, similarity)
    x = x + jnp.tanh(g_xattn[0]) * _L0_xattn_ref(ctx_512, _layernorm(x, axis=-1), L0_xattn_W, L0_xattn_b)
    x = x + jnp.tanh(g_ffn[0]) * _L0_ffn_ref(_layernorm(x, axis=-1), L0_ffn_gate_weight, L0_ffn_gate_up_proj, L0_ffn_down_proj, L0_ffn_similarity)
    return x

_drawn_inputs = setup_inputs


def setup_inputs(seed=0):
    import zlib

    import numpy as np

    out = dict(_drawn_inputs(seed))
    spreads = {}
    factors = {'L0_ffn_gate_weight': 3.798,
     'L0_ffn_gate_up_proj': 3.52,
     'L0_ffn_down_proj': 3.529,
     'L0_ffn_similarity': 8.0}
    for name, (base, spread) in spreads.items():
        noise = np.random.default_rng([zlib.crc32(name.encode()), seed]).standard_normal(out[name].shape)
        drawn = base * np.exp(spread * noise) if base else spread * noise
        out[name] = jnp.asarray(drawn.astype(out[name].dtype))
    for name, factor in factors.items():
        out[name] = (out[name] * factor).astype(out[name].dtype)
    return out
```

```python
from contextlib import ExitStack

import numpy as np
import concourse.bass as bass
from concourse import mybir

ALU = mybir.AluOpType
ACT = mybir.ActivationFunctionType
AX = mybir.AxisListType
F32 = mybir.dt.float32
F16 = mybir.dt.float16
I32 = mybir.dt.int32
U32 = mybir.dt.uint32

P = 128
TOPK = 8
PRIM = 4
THRESHOLD = 0.5
P_ASEM = 0.6
EPS = 1e-5
W_BUFS = 4


def build(nc, x, ctxT, W, b, g_xattn, g_ffn, gwT, wupT, wdnT, sim, out):
    B, N, D = x.shape
    DC = ctxT.shape[1]
    E = gwT.shape[1]
    F = wupT.shape[2] * P // (2 * D)
    KC = D // P
    FC = 2
    FP = F // FC
    TB = N // P
    TOK = B * N
    NT = TOK // P
    TILES = (TOK * TOPK + E * (P - 1)) // P
    PAIRS = (TILES + 1) // 2
    TABLE = 2 * PAIRS + 4
    ROW = D + E
    assert DC == P and D % P == 0 and FP <= P and PRIM * E == P and E == 32 and W_BUFS == 4

    x_v = x.rearrange("b (t p) d -> b p t d", p=P)
    out_v = out.rearrange("(t p) d -> p t d", p=P)
    scratch = nc.dram_tensor("token_rows", [TOK + P, ROW], F32, kind="Internal").ap()
    scratch_v = scratch.rearrange("(t p) d -> p t d", p=P)

    with ExitStack() as ctx:
        def sb(name, shape, dt=F32):
            return ctx.enter_context(nc.sbuf_tensor(name, shape, dt))

        def ps(name, shape, dt=F32):
            return ctx.enter_context(nc.psum_tensor(name, shape, dt))

        def sem(name):
            return ctx.enter_context(nc.semaphore(name))

        ident = sb("ident", [P, P])
        ones = sb("ones", [P, P])
        ones16 = sb("ones16", [P, P], F16)
        before = sb("before", [P, P], F16)
        iota_e = sb("iota_e", [P, E])
        iota_tile = sb("iota_tile", [P, TABLE])
        token_id1 = sb("token_id1", [P, NT])
        pad_id1 = sb("pad_id1", [P, 1])
        prim_order = sb("prim_order", [P, PRIM])
        gates = sb("gates", [1, 3])
        w_ij = sb("w_ij", [P, 2])
        ctx_sb = sb("ctx_sb", [P, B, N])
        gw_sb = sb("gw_sb", [P, KC, E])
        sim_bd = sb("sim_bd", [P, P])
        xs = sb("xs", [P, NT, D])
        wj_rep = sb("wj_rep", [P, P])
        gate_col = sb("gate_col", [P, 3])
        c_sig = sb("c_sig", [P, 1])
        c_ln = sb("c_ln", [P, 1])
        c_lnn = sb("c_lnn", [P, 1])
        si_b = sb("si_b", [P, NT])
        sig = sb("sig", [P, NT, N])
        eps_col = sb("eps_col", [P, 1])
        stats = sb("stats", [P, 2, NT, 6])
        mv = sb("mv", [P, 2, NT, 2])
        std = sb("std", [P, 2, NT])
        rstd = sb("rstd", [P, 2, NT])
        ln_a = sb("ln_a", [P, NT])
        ln_b = sb("ln_b", [P, NT])
        ln2_b = sb("ln2_b", [P, NT])
        rows_sb = sb("rows_sb", [P, NT, ROW])
        xnT = sb("xnT", [P, 2, D])
        rmax = sb("rmax", [P, TB])
        probs = sb("probs", [P, TB, E])
        exps = sb("exps", [P, TB, E])
        rsum = sb("rsum", [P, TB])
        rrec = sb("rrec", [P, TB])
        top = sb("top", [P, TB, TOPK])
        topi = sb("topi", [P, TB, TOPK], U32)
        topf = sb("topf", [P, TB, TOPK])
        oh = sb("oh", [P, NT, TOPK, E])
        wts = sb("wts", [P, TB, TOPK])
        wfin = sb("wfin", [P, NT, TOPK])
        ohT = sb("ohT", [P, TB, P])
        cmul = ctx_sb[:].rearrange("p b n -> p (b n)")[:, 0:TB * PRIM * PRIM * E].rearrange(
            "p (t c e) -> p t c e", c=PRIM * PRIM, e=E)
        cand = sb("cand", [P, TB * PRIM, PRIM])
        best = sb("best", [P, TB * PRIM])
        eqb = sb("eqb", [P, TB * PRIM, PRIM])
        eqm = sb("eqm", [P, TB * PRIM])
        wgo = sb("wgo", [P, TB, PRIM])
        wadd = sb("wadd", [P, TB, PRIM])
        ohw = sb("ohw", [P, TB * TOPK, E])
        comb = sb("comb", [P, TB, E])
        mask = sb("mask", [P, NT, E], F16)
        cnt_i = sb("cnt_i", [E, 1], I32)
        nt_i = sb("nt_i", [E, 1], I32)
        nt_f = sb("nt_f", [E, 1])
        nt_rep = sb("nt_rep", [E, P], F16)
        base128 = sb("base128", [P, E])
        end_col = sb("end_col", [E, 1])
        end_ge = sb("end_ge", [E, TABLE], F16)
        expert_tab = sb("expert_tab", [P, TABLE])
        expert_i = sb("expert_i", [1, TABLE], I32)
        end_i = sb("end_i", [1, E], I32)
        pairs_i = sb("pairs_i", [1, 2], I32)
        slot_e = sb("slot_e", [P, NT, E])
        free = sig[:].rearrange("p t n -> p (t n)")
        used = [0]

        def reuse(*shape):
            size = int(np.prod(shape))
            part = free[:, used[0]:used[0] + size]
            used[0] += size
            names = "abc"[:len(shape)]
            return part.rearrange(f"p ({' '.join(names)}) -> p {' '.join(names)}", **dict(zip(names[1:], shape[1:])))

        slot_m = reuse(NT, TOPK, E)
        slot_r = sb("slot_r", [P, NT * TOPK])
        slot_i = sb("slot_i", [P, NT * TOPK], I32)
        srow_i = sb("srow_i", [P, NT * TOPK], I32)
        stile_i = sb("stile_i", [P, NT * TOPK], I32)
        srow = sb("srow", [P, NT * TOPK])
        stile = sb("stile", [P, NT * TOPK])
        valid = sb("valid", [P, NT * TOPK])
        hit_row = sb("hit_row", [P, 2, TOPK, P], F16)
        hit_tile = sb("hit_tile", [P, 2, TOPK, TABLE], F16)
        tab_f = sb("tab_f", [P, TABLE])
        token_tab = sb("token_tab", [P, TABLE], I32)
        wup = sb("wup", [P, W_BUFS, KC * 2 * F])
        wdn = sb("wdn", [FP, W_BUFS, FC * D])
        g_idx = sb("g_idx", [P, 2], I32)
        s_idx = sb("s_idx", [P, 2], I32)
        gath = reuse(2, ROW)
        xT = reuse(2, KC, P)
        wsel = sb("wsel", [P, E])
        slot_w = sb("slot_w", [P, 2])
        silu_g = reuse(2, F)
        hid = reuse(2, F)
        hidT = sb("hidT", [FP, 2, FC, P])
        ysb = reuse(2, D)
        zrow = sb("zrow", [P, ROW])
        turn = sb("turn", [1, 1])

        bank = [ps(f"bank{i}", [P, 512]) for i in range(8)]

        inputs_in = sem("inputs_in")
        router_in = sem("router_in")
        x_in = [sem(f"x_in{i}") for i in range(B)]
        consts = sem("consts")
        cfix = sem("cfix")
        gates_ps = sem("gates_ps")
        tanh_done = sem("tanh_done")
        bcol_done = sem("bcol_done")
        wjrep_done = sem("wjrep_done")
        si_ps = sem("si_ps")
        sib_done = sem("sib_done")
        sj_ps = sem("sj_ps")
        sig_done = sem("sig_done")
        var_done = sem("var_done")
        std_done = sem("std_done")
        lnab_done = sem("lnab_done")
        t1_done = sem("t1_done")
        x1_done = sem("x1_done")
        ln2_done = sem("ln2_done")
        xn_done = sem("xn_done")
        xnT_ps = sem("xnT_ps")
        xnT_done = sem("xnT_done")
        logit_ps = sem("logit_ps")
        shift_done = sem("shift_done")
        exp_done = sem("exp_done")
        oh_done = sem("oh_done")
        ohT_ps = sem("ohT_ps")
        ohT_done = sem("ohT_done")
        simrow_ps = sem("simrow_ps")
        simrow_used = sem("simrow_used")
        mask_done = sem("mask_done")
        combrow_done = sem("combrow_done")
        pos_ps = sem("pos_ps")
        ntrep_done = sem("ntrep_done")
        base_ps = sem("base_ps")
        endge_done = sem("endge_done")
        etab_ps = sem("etab_ps")
        regs_done = sem("regs_done")
        hits_done = sem("hits_done")
        hits_used = sem("hits_used")
        table_ps = sem("table_ps")
        table_done = sem("table_done")
        chain = sem("chain")
        x1_stored = sem("x1_stored")
        rows_stored = sem("rows_stored")
        w_loaded = sem("w_loaded")
        out_added = sem("out_added")
        idx_staged = sem("idx_staged")
        sidx_staged = sem("sidx_staged")
        gath_in = [sem("gath_in0"), sem("gath_in1")]
        slotx_ps = sem("slotx_ps")
        slotx_done = sem("slotx_done")
        gu_ps = sem("gu_ps")
        silu_done = sem("silu_done")
        hid_done = sem("hid_done")
        hidT_ps = sem("hidT_ps")
        hidT_done = sem("hidT_done")
        y_ps = sem("y_ps")
        ybank_free = sem("ybank_free")
        y_done = sem("y_done")
        wsel_done = sem("wsel_done")
        slotw_done = sem("slotw_done")

        block = ctx.enter_context(nc.Block())

        def load_expert(sp, e, buf):
            sp.dma_start(wup[:, buf, :], wupT[e]).then_inc(w_loaded, 16)
            sp.dma_start(wdn[:, buf, :], wdnT[e]).then_inc(w_loaded, 16)

        @block.sync
        def _(sp):
            sp.dma_start(gates[:, 0:1], b).then_inc(inputs_in, 16)
            sp.dma_start(gates[:, 1:2], g_xattn).then_inc(inputs_in, 16)
            sp.dma_start(gates[:, 2:3], g_ffn).then_inc(inputs_in, 16)
            sp.dma_start(w_ij[:], W).then_inc(inputs_in, 16)
            sp.dma_start(ctx_sb[:], ctxT.rearrange("b d n -> d b n")).then_inc(inputs_in, 16)
            for q in range(B):
                sp.dma_start(xs[:, q * TB:(q + 1) * TB, :], x_v[q]).then_inc(x_in[q], 16)
                if q == 0:
                    sp.dma_start(gw_sb[:], gwT.rearrange("(c p) e -> p c e", p=P)).then_inc(router_in, 16)
                    sp.wait_ge(consts, 1)
                    for k in range(PRIM):
                        sp.dma_start(sim_bd[E * k:E * (k + 1), E * k:E * (k + 1)], sim).then_inc(router_in, 16)
            for e in range(W_BUFS):
                load_expert(sp, e, e)
                sp.wait_ge(w_loaded, 32 * (e + 1))
                if e < B:
                    sp.wait_ge(x1_done, TB * (e + 1))
                    sp.dma_start(out_v[:, e * TB:(e + 1) * TB, :], xs[:, e * TB:(e + 1) * TB, :]).then_inc(x1_stored, 16)
            for q in range(B):
                sp.wait_ge(combrow_done, q + 1)
                sp.dma_start(scratch_v[:, q * TB:(q + 1) * TB, :],
                             rows_sb[:, q * TB:(q + 1) * TB, :]).then_inc(rows_stored, 16)
            sp.wait_ge(regs_done, 3)
            with sp.Fori(1, E // W_BUFS) as k:
                for j in range(W_BUFS):
                    end = sp.value_load(end_i[0:1, bass.ds(W_BUFS * (k - 1) + j, 1)], min_val=0, max_val=TILES)
                    sp.wait_ge(y_ps, end + 1)
                    sp.wait_ge(w_loaded, 32 * (W_BUFS * k + j))
                    load_expert(sp, W_BUFS * k + j, j)
            sp.wait_ge(w_loaded, 32 * E)

        @block.gpsimd
        def _(pool):
            pool.memset(sim_bd[:], 0.0).then_inc(consts, 1)
            pool.memset(ident[:], 0.0).then_inc(cfix, 1)
            pool.memset(before[:], 1.0).then_inc(cfix, 1)
            pool.memset(ones[:], 1.0).then_inc(consts, 1)
            pool.memset(ones16[:], 1.0).then_inc(consts, 1)
            pool.wait_ge(cfix, 2)
            pool.affine_select(out=ident[:], in_=ident[:], compare_op=ALU.not_equal, fill=1.0, base=0,
                               pattern=[[-1, P]], channel_multiplier=1).then_inc(consts, 1)
            pool.affine_select(out=before[:], in_=before[:], compare_op=ALU.is_gt, fill=0.0, base=0,
                               pattern=[[1, P]], channel_multiplier=-1).then_inc(consts, 1)
            exact = dict(allow_small_or_imprecise_dtypes=True)
            pool.iota(iota_e[:], [[1, E]], 0, 0, **exact).then_inc(consts, 1)
            pool.iota(iota_tile[:], [[1, TABLE]], 0, 0, **exact).then_inc(consts, 1)
            pool.iota(token_id1[:], [[P, NT]], 1, 1, **exact).then_inc(consts, 1)
            pool.iota(pad_id1[:], [[0, 1]], TOK + 1, 1, **exact).then_inc(consts, 1)
            pool.iota(prim_order[:], [[-1, PRIM]], PRIM, 0, **exact).then_inc(consts, 1)
            pool.memset(zrow[:], 0.0).then_inc(consts, 1)
            pool.memset(eps_col[:], EPS).then_inc(consts, 1)
            pool.wait_ge(router_in, 16 * (1 + PRIM))
            pool.affine_select(out=sim_bd[:], in_=sim_bd[:], compare_op=ALU.not_equal, fill=1.0, base=0,
                               pattern=[[-1, P]], channel_multiplier=1).then_inc(consts, 1)
            pool.wait_ge(consts, 12)
            pool.dma_start(scratch_v[:, NT, :], zrow[:]).then_inc(out_added, 16)
            pool.dma_start(out_v[:, NT, :], zrow[:, 0:D]).then_inc(out_added, 16)

            def settle():
                pool.tensor_tensor(turn[:], zrow[0:1, 0:1], zrow[0:1, 0:1], ALU.add)

            def gather(i, buf):
                pool.tensor_copy(g_idx[:, buf:buf + 1], token_tab[:, bass.ds(i, 1)]).then_inc(idx_staged, 1)
                pool.wait_ge(idx_staged, i + 1)
                settle()
                pool.indirect_dma_start(
                    out=gath[:, buf, :], out_offset=None, in_=scratch,
                    in_offset=bass.IndirectOffsetOnAxis(ap=g_idx[:, buf:buf + 1], axis=0),
                ).then_inc(gath_in[buf], 16)

            pool.wait_ge(table_done, 1)
            pool.wait_ge(rows_stored, 16 * B)
            pool.wait_ge(x1_stored, 16 * B)
            pool.wait_ge(out_added, 32)
            gather(0, 0)
            gather(1, 1)
            pool.wait_ge(slotx_ps, 1)
            pool.wait_ge(slotw_done, 1)
            pool.wait_ge(gath_in[0], 16)
            gather(2, 0)
            pairs = pool.value_load(pairs_i[0:1, 1:2], min_val=1, max_val=PAIRS)
            with pool.Fori(0, PAIRS) as g:
                with pool.If(g < pairs):
                    for u in range(2):
                        i = 2 * g + u
                        pool.wait_ge(slotx_ps, i + 2)
                        pool.wait_ge(slotw_done, i + 2)
                        pool.wait_ge(gath_in[1 - u], 16 * (g + 1 + u))
                        gather(i + 3, 1 - u)
                        pool.wait_ge(out_added, 16 * (i + 2))
                        pool.tensor_copy(s_idx[:, u:u + 1], token_tab[:, bass.ds(i, 1)]).then_inc(sidx_staged, 1)
                        pool.wait_ge(sidx_staged, i + 1)
                        pool.wait_ge(y_done, i + 1)
                        settle()
                        pool.indirect_dma_start(
                            out=out, out_offset=bass.IndirectOffsetOnAxis(ap=s_idx[:, u:u + 1], axis=0),
                            in_=ysb[:, u, :], in_offset=None, compute_op=ALU.add,
                        ).then_inc(out_added, 16)
            pool.wait_ge(out_added, 32 * pairs + 32)
            pool.wait_ge(gath_in[0], 16 * pairs + 32)
            pool.wait_ge(gath_in[1], 16 * pairs + 16)

        @block.scalar
        def _(act):
            act.wait_ge(gates_ps, 1)
            act.activation(gate_col[:, 1:3], bank[0][:, 1:3], ACT.Tanh).then_inc(tanh_done, 1)
            act.wait_ge(sib_done, 1)
            for q in range(B):
                act.wait_ge(sj_ps, q + 1)
                for t in range(TB):
                    n = q * TB + t
                    act.activation(sig[:, n, :], bank[2 + q % 2][:], ACT.Sigmoid,
                                   bias=si_b[:, n:n + 1]).then_inc(sig_done, 1)

            def add_norm(q):
                for n in range(q * TB, (q + 1) * TB):
                    act.activation(xs[:, n, :], xs[:, n, :], ACT.Identity, bias=ln_b[:, n:n + 1],
                                   scale=ln_a[:, n:n + 1]).then_inc(t1_done, 1)

            act.wait_ge(consts, 13)
            act.wait_ge(var_done, 1)
            act.activation(std[:, 0, :], mv[:, 0, :, 1], ACT.Sqrt, bias=eps_col[:]).then_inc(std_done, 1)
            act.wait_ge(lnab_done, 1)
            add_norm(0)
            for q in range(B):
                if q + 1 < B:
                    add_norm(q + 1)
                act.wait_ge(var_done, q + 2)
                act.activation(std[:, 1, q * TB:(q + 1) * TB], mv[:, 1, q * TB:(q + 1) * TB, 1], ACT.Sqrt,
                               bias=eps_col[:]).then_inc(std_done, 1)
                act.wait_ge(ln2_done, q + 1)
                for n in range(q * TB, (q + 1) * TB):
                    act.activation(rows_sb[:, n, 0:D], xs[:, n, :], ACT.Identity, bias=ln2_b[:, n:n + 1],
                                   scale=rstd[:, 1, n:n + 1]).then_inc(xn_done, 1)
                for n in range(q * TB, (q + 1) * TB):
                    act.wait_ge(xnT_ps, n + 1)
                    if n >= 2:
                        act.wait_ge(logit_ps, n - 1)
                    act.activation(xnT[:, n % 2, :], bank[4 + n % 2][:], ACT.Copy).then_inc(xnT_done, 1)
            for q in range(B):
                act.wait_ge(shift_done, q + 1)
                if q >= 1:
                    act.wait_ge(mask_done, q)
                act.activation(exps[:], probs[:], ACT.Exp).then_inc(exp_done, 1)
                act.wait_ge(ohT_ps, q + 1)
                act.activation(ohT[:].rearrange("p t c -> p (t c)"), bank[6][:], ACT.Copy).then_inc(ohT_done, 1)

            def evacuate_x(i, buf):
                act.wait_ge(slotx_ps, i + 1)
                act.activation(xT[:, buf].rearrange("p c n -> p (c n)"), bank[buf][:],
                               ACT.Copy).then_inc(slotx_done, 1)

            def silu(i, buf):
                act.wait_ge(gu_ps, i + 1)
                act.activation(silu_g[:, buf, :], bank[2 + buf][:, 0:F], ACT.Silu).then_inc(silu_done, 1)

            evacuate_x(0, 0)
            evacuate_x(1, 1)
            silu(0, 0)
            act.wait_ge(regs_done, 3)
            pairs = act.value_load(pairs_i[0:1, 1:2], min_val=1, max_val=PAIRS)
            with act.Fori(0, PAIRS) as g:
                with act.If(g < pairs):
                    for u in range(2):
                        i = 2 * g + u
                        act.wait_ge(hid_done, i + 1)
                        silu(i + 1, 1 - u)
                        evacuate_x(i + 2, u)

        @block.vector
        def _(dve):
            steps = [0]

            def after(ins):
                steps[0] += 1
                ins.then_inc(chain, 1)
                dve.wait_ge(chain, steps[0])

            dve.wait_ge(consts, 2)
            dve.wait_ge(inputs_in, 16 * 5)
            dve.tensor_scalar(wj_rep[:], ones[:], w_ij[:, 1:2], None, ALU.mult).then_inc(wjrep_done, 1)
            dve.wait_ge(tanh_done, 1)
            dve.tensor_copy(gate_col[:, 0:1], bank[0][:, 0:1]).then_inc(bcol_done, 1)
            dve.wait_ge(bcol_done, 1)
            dve.wait_ge(si_ps, 1)
            dve.tensor_scalar(si_b[:], bank[1][:, 0:NT], gate_col[:, 0:1], None, ALU.add).then_inc(sib_done, 1)
            dve.wait_ge(tanh_done, 1)
            dve.tensor_scalar(c_sig[:], gate_col[:, 1:2], P_ASEM, None, ALU.mult)
            dve.tensor_scalar(c_ln[:], gate_col[:, 1:2], 1.0 - P_ASEM, None, ALU.mult)
            after(dve.tensor_scalar(c_lnn[:], gate_col[:, 1:2], P_ASEM - 1.0, None, ALU.mult))
            dve.wait_ge(consts, 13)

            def moments(which, tiles, signals):
                for n in tiles:
                    if which == 0 and n % TB == 0:
                        dve.wait_ge(x_in[n // TB], 16)
                    ins = dve.bn_stats(stats[:, which, n, :], xs[:, n, :])
                after(ins)
                for n in tiles:
                    ins = dve.bn_aggr(mv[:, which, n, :], stats[:, which, n, :])
                ins.then_inc(var_done, 1)
                dve.wait_ge(std_done, signals)
                after(dve.reciprocal(rstd[:, which, tiles[0]:tiles[-1] + 1], std[:, which, tiles[0]:tiles[-1] + 1]))

            moments(0, range(NT), 1)
            after(dve.tensor_scalar(ln_a[:], rstd[:, 0, :], c_ln[:], 1.0, ALU.mult, ALU.add))
            dve.scalar_tensor_tensor(out=ln_b[:], in0=mv[:, 0, :, 0], scalar=c_lnn[:],
                                     in1=rstd[:, 0, :], op0=ALU.mult, op1=ALU.mult).then_inc(lnab_done, 1)
            for q in range(B):
                n0, n1 = q * TB, (q + 1) * TB
                for n in range(n0, n1):
                    dve.wait_ge(t1_done, n + 1)
                    dve.wait_ge(sig_done, n + 1)
                    dve.scalar_tensor_tensor(out=xs[:, n, :], in0=sig[:, n, :], scalar=c_sig[:], in1=xs[:, n, :],
                                             op0=ALU.mult, op1=ALU.add).then_inc(x1_done, 1)
                dve.wait_ge(x1_done, n1)
                moments(1, range(n0, n1), q + 2)
                dve.scalar_tensor_tensor(out=ln2_b[:, n0:n1], in0=mv[:, 1, n0:n1, 0], scalar=-1.0,
                                         in1=rstd[:, 1, n0:n1], op0=ALU.mult, op1=ALU.mult).then_inc(ln2_done, 1)

            def spread(v, n):
                return v.unsqueeze(2).broadcast_to([v.shape[0], v.shape[1], n])

            def route(q):
                n0, n1 = q * TB, (q + 1) * TB
                dve.wait_ge(logit_ps, n1)
                logits = bank[q][:, 0:TB * E].rearrange("p (t e) -> p t e", e=E)
                after(dve.tensor_reduce(rmax[:], logits, AX.X, ALU.max))
                dve.tensor_tensor(probs[:], logits, spread(rmax[:], E), ALU.subtract).then_inc(shift_done, 1)
                dve.wait_ge(exp_done, q + 1)
                after(dve.tensor_reduce(rsum[:], exps[:], AX.X, ALU.add))
                after(dve.reciprocal(rrec[:], rsum[:]))
                after(dve.tensor_tensor(probs[:], exps[:], spread(rrec[:], E), ALU.mult))
                for t in range(TB):
                    ins = dve.max(top[:, t, :], probs[:, t, :])
                after(ins)
                for t in range(TB):
                    ins = dve.max_index(topi[:, t, :], top[:, t, :], probs[:, t, :])
                after(ins)
                after(dve.tensor_copy(topf[:], topi[:]))
                ohq = oh[:, n0:n1].rearrange("p t r e -> p (t r) e")
                dve.tensor_tensor(ohq, spread(topf[:].rearrange("p t r -> p (t r)"), E),
                                  iota_e[:].unsqueeze(1).broadcast_to([P, TB * TOPK, E]),
                                  ALU.is_equal).then_inc(oh_done, 1)
                after(dve.tensor_reduce(rsum[:], top[:], AX.X, ALU.add))
                after(dve.tensor_scalar(rsum[:], rsum[:], 1e-12, None, ALU.max))
                after(dve.reciprocal(rrec[:], rsum[:]))
                after(dve.tensor_tensor(wts[:], top[:], spread(rrec[:], TOPK), ALU.mult))
                dve.wait_ge(simrow_ps, q + 1)
                for t in range(TB):
                    rows = bank[6][:, t * P:(t + 1) * P].rearrange("p (k e) -> p k e", e=E)
                    rows = rows.unsqueeze(2).broadcast_to([P, PRIM, PRIM, E])
                    prim = oh[:, n0 + t, 0:PRIM, :].unsqueeze(1).broadcast_to([P, PRIM, PRIM, E])
                    ins = dve.tensor_tensor(cmul[:, t].rearrange("p (k j) e -> p k j e", j=PRIM), rows, prim, ALU.mult)
                ins.then_inc(simrow_used, 1)
                dve.wait_ge(simrow_used, q + 1)
                after(dve.tensor_reduce(cand[:].rearrange("p k j -> p (k j)"),
                                        cmul.rearrange("p t c e -> p (t c) e"), AX.X, ALU.add))
                after(dve.tensor_reduce(best[:], cand[:], AX.X, ALU.max))
                after(dve.tensor_tensor(eqb[:], cand[:], spread(best[:], PRIM), ALU.is_equal))
                after(dve.tensor_tensor(eqb[:], eqb[:], prim_order[:].unsqueeze(1).broadcast_to([P, TB * PRIM, PRIM]),
                                        ALU.mult))
                after(dve.tensor_reduce(eqm[:], eqb[:], AX.X, ALU.max))
                after(dve.tensor_tensor(eqb[:], eqb[:], spread(eqm[:], PRIM), ALU.is_equal))
                best_t = best[:].rearrange("p (t k) -> p t k", k=PRIM)
                dve.scalar_tensor_tensor(out=wfin[:, n0:n1, PRIM:], in0=best_t, scalar=THRESHOLD,
                                         in1=wts[:, :, PRIM:], op0=ALU.is_lt, op1=ALU.mult)
                after(dve.scalar_tensor_tensor(out=wgo[:], in0=best_t, scalar=THRESHOLD, in1=wts[:, :, PRIM:],
                                               op0=ALU.is_ge, op1=ALU.mult))
                after(dve.tensor_tensor(eqb[:], eqb[:], spread(wgo[:].rearrange("p t k -> p (t k)"), PRIM), ALU.mult))
                after(dve.tensor_reduce(wadd[:], eqb[:].rearrange("p (t k) j -> p t j k", k=PRIM), AX.X, ALU.add))
                after(dve.tensor_tensor(wfin[:, n0:n1, 0:PRIM], wts[:, :, 0:PRIM], wadd[:], ALU.add))
                after(dve.tensor_tensor(ohw[:], ohq, spread(wfin[:, n0:n1].rearrange("p t r -> p (t r)"), E), ALU.mult))
                after(dve.tensor_reduce(comb[:], ohw[:].rearrange("p (t r) e -> p t e r", r=TOPK), AX.X, ALU.add))
                dve.tensor_scalar(mask[:, n0:n1, :], comb[:], 0.0, None, ALU.is_gt).then_inc(mask_done, 1)
                dve.wait_ge(xn_done, n1)
                dve.tensor_scalar(rows_sb[:, n0:n1, D:], comb[:], gate_col[:, 2:3], None,
                                  ALU.mult).then_inc(combrow_done, 1)

            for q in range(B):
                route(q)

            dve.wait_ge(pos_ps, 1)
            after(dve.tensor_scalar(cnt_i[:], bank[1][0:E, 0:1], float(P - 1), None, ALU.add))
            after(dve.tensor_scalar(nt_i[:], cnt_i[:], 7, None, ALU.arith_shift_right))
            after(dve.tensor_copy(nt_f[:], nt_i[:]))
            dve.tensor_scalar(nt_rep[:], ones[0:E, :], nt_f[:], None, ALU.mult).then_inc(ntrep_done, 1)
            dve.wait_ge(base_ps, 1)
            dve.tensor_copy(end_col[:], bank[1][0:E, 1:2])
            dve.tensor_copy(end_i[:], bank[1][0:1, 65:65 + E]).then_inc(regs_done, 1)
            dve.tensor_scalar(pairs_i[:, 0:1], bank[1][0:1, 64 + E:65 + E], 1.0, None, ALU.add)
            after(dve.tensor_scalar(base128[:], bank[1][:, 64:64 + E], float(P), None, ALU.mult))
            dve.tensor_scalar(pairs_i[:, 1:2], pairs_i[:, 0:1], 1, None, ALU.arith_shift_right).then_inc(regs_done, 1)
            dve.tensor_scalar(end_ge[:], iota_tile[0:E, :], end_col[:], None, ALU.is_ge).then_inc(endge_done, 1)
            after(dve.tensor_tensor(slot_e[:], bank[0][:].rearrange("p (t e) -> p t e", e=E),
                                    base128[:].unsqueeze(1).broadcast_to([P, NT, E]), ALU.add))
            dve.tensor_scalar(valid[:], wfin[:].rearrange("p t r -> p (t r)"), 0.0, None, ALU.is_gt)
            for n in range(NT):
                ins = dve.tensor_tensor(slot_m[:, n], oh[:, n],
                                        slot_e[:, n].unsqueeze(1).broadcast_to([P, TOPK, E]), ALU.mult)
            after(ins)
            after(dve.tensor_reduce(slot_r[:], slot_m.rearrange("p t r e -> p (t r) e"), AX.X, ALU.add))
            after(dve.scalar_tensor_tensor(out=slot_r[:], in0=slot_r[:], scalar=1.0, in1=valid[:],
                                           op0=ALU.add, op1=ALU.mult))
            after(dve.tensor_scalar(slot_i[:], slot_r[:], -1.0, None, ALU.add))
            dve.tensor_scalar(srow_i[:], slot_i[:], P - 1, None, ALU.bitwise_and)
            after(dve.tensor_scalar(stile_i[:], slot_i[:], 7, None, ALU.arith_shift_right))
            dve.tensor_copy(srow[:], srow_i[:])
            after(dve.tensor_copy(stile[:], stile_i[:]))
            dve.wait_ge(etab_ps, 1)
            dve.tensor_copy(expert_i[:], bank[2][0:1, 0:TABLE]).then_inc(regs_done, 1)
            dve.tensor_copy(expert_tab[:], bank[2][:, 0:TABLE])

            def hits(n, buf):
                dve.tensor_tensor(hit_row[:, buf], spread(srow[:, bass.ds(n * TOPK, TOPK)], P),
                                  iota_tile[:, 0:P].unsqueeze(1).broadcast_to([P, TOPK, P]), ALU.is_equal)
                for r in range(TOPK):
                    ins = dve.tensor_scalar(hit_tile[:, buf, r, :], iota_tile[:],
                                            stile[:, bass.ds(n * TOPK + r, 1)], token_id1[:, bass.ds(n, 1)],
                                            ALU.is_equal, ALU.mult)
                ins.then_inc(hits_done, 1)

            hits(0, 0)
            hits(1, 1)
            with dve.Fori(1, NT // 2) as g:
                for u in range(2):
                    dve.wait_ge(hits_used, 2 * g + u - 1)
                    hits(2 * g + u, u)
            dve.wait_ge(table_ps, 1)
            after(dve.tensor_scalar(tab_f[:], bank[3][:, 0:TABLE], 0.0, pad_id1[:], ALU.is_equal, ALU.mult))
            dve.scalar_tensor_tensor(out=token_tab[:], in0=bank[3][:, 0:TABLE], scalar=-1.0, in1=tab_f[:],
                                     op0=ALU.add, op1=ALU.add).then_inc(table_done, 1)

            def weigh(i, buf, arrived):
                dve.wait_ge(gath_in[buf], arrived)
                dve.scalar_tensor_tensor(out=wsel[:], in0=iota_e[:], scalar=expert_tab[:, bass.ds(i, 1)],
                                         in1=gath[:, buf, D:], op0=ALU.is_equal, op1=ALU.mult).then_inc(wsel_done, 1)
                dve.wait_ge(wsel_done, i + 1)
                dve.tensor_reduce(slot_w[:, buf:buf + 1], wsel[:], AX.X, ALU.add).then_inc(slotw_done, 1)

            def hidden(i, buf):
                dve.wait_ge(silu_done, i + 1)
                dve.tensor_tensor(hid[:, buf, :], silu_g[:, buf, :], bank[2 + buf][:, F:2 * F],
                                  ALU.mult).then_inc(hid_done, 1)

            weigh(0, 0, 16)
            hidden(0, 0)
            dve.sem_inc(ybank_free, 2)
            pairs = dve.value_load(pairs_i[0:1, 1:2], min_val=1, max_val=PAIRS)
            with dve.Fori(0, PAIRS) as g:
                with dve.If(g < pairs):
                    for u in range(2):
                        i = 2 * g + u
                        dve.wait_ge(hidT_ps, i + 1)
                        dve.tensor_copy(hidT[:, u].rearrange("p c n -> p (c n)"),
                                        bank[4][0:FP, 0:FC * P]).then_inc(hidT_done, 1)
                        hidden(i + 1, 1 - u)
                        weigh(i + 1, 1 - u, 16 * (g + 1))
                        dve.wait_ge(y_ps, i + 2)
                        dve.wait_ge(out_added, 16 * (i + 1))
                        dve.tensor_scalar(ysb[:, u, :], bank[5 + u][:], slot_w[:, u:u + 1], None,
                                          ALU.mult).then_inc(y_done, 1)
                        dve.wait_ge(y_done, i + 1)
                        dve.sem_inc(ybank_free, 1)

        @block.tensor
        def _(pe):
            pe.wait_ge(consts, 2)
            pe.wait_ge(inputs_in, 16 * 5)
            pe.matmul(bank[0][:, 0:3], ones[0:1, :], gates[:], start=True, stop=True).then_inc(gates_ps, 1)
            for n in range(NT):
                q, t = divmod(n, TB)
                mm = pe.matmul(bank[1][:, n:n + 1], ctx_sb[:, q, t * P:(t + 1) * P], w_ij[:, 0:1], start=True, stop=True)
            mm.then_inc(si_ps, 1)
            pe.wait_ge(wjrep_done, 1)
            for q in range(B):
                if q >= 2:
                    pe.wait_ge(sig_done, TB * (q - 1))
                pe.matmul(bank[2 + q % 2][:], wj_rep[:], ctx_sb[:, q, :], start=True, stop=True).then_inc(sj_ps, 1)
            pe.wait_ge(consts, 4)
            pe.wait_ge(router_in, 16 * (1 + PRIM))

            def similar(q):
                pe.wait_ge(oh_done, q + 1)
                if q >= 1:
                    pe.wait_ge(simrow_used, q)
                for t in range(TB):
                    mm = pe.transpose(bank[6][:, t * P:(t + 1) * P],
                                      oh[:, q * TB + t, PRIM:, :].rearrange("p k e -> p (k e)"), ident[:])
                mm.then_inc(ohT_ps, 1)
                pe.wait_ge(consts, 13)
                pe.wait_ge(ohT_done, q + 1)
                for t in range(TB):
                    mm = pe.matmul(bank[6][:, t * P:(t + 1) * P], ohT[:, t, :], sim_bd[:], start=True, stop=True)
                mm.then_inc(simrow_ps, 1)

            def xn_transpose(n):
                pe.wait_ge(xn_done, n + 1)
                if n >= 2:
                    pe.wait_ge(xnT_done, n - 1)
                for c in range(KC):
                    mm = pe.transpose(bank[4 + n % 2][:, c * P:(c + 1) * P], rows_sb[:, n, c * P:(c + 1) * P], ident[:])
                mm.then_inc(xnT_ps, 1)

            def logits(n):
                pe.wait_ge(xnT_done, n + 1)
                for c in range(KC):
                    mm = pe.matmul(bank[n // TB][:, n % TB * E:(n % TB + 1) * E], xnT[:, n % 2, c * P:(c + 1) * P], gw_sb[:, c, :],
                                   start=(c == 0), stop=(c == KC - 1))
                mm.then_inc(logit_ps, 1)

            for q in range(B):
                xn_transpose(q * TB)
                for t in range(TB):
                    n = q * TB + t
                    if t + 1 < TB:
                        xn_transpose(n + 1)
                    logits(n)
            for q in range(B):
                similar(q)

            pe.wait_ge(mask_done, B)
            allm = mask[:].rearrange("p t e -> p (t e)")
            pe.matmul(bank[0][:], before[:], allm, start=True, stop=False, skip_group_check=True)
            for n in range(NT - 1):
                pe.matmul(bank[0][:, (n + 1) * E:].rearrange("p (t e) -> p t e", e=E), ones16[:],
                          mask[:, n, :].unsqueeze(1).broadcast_to([P, NT - 1 - n, E]),
                          start=False, stop=(n == NT - 2), skip_group_check=True)
            for n in range(NT):
                mm = pe.matmul(bank[1][0:E, 0:1], mask[:, n, :], ones16[:, 0:1], start=(n == 0), stop=(n == NT - 1))
            mm.then_inc(pos_ps, 1)
            pe.wait_ge(ntrep_done, 1)
            pe.matmul(bank[1][0:E, 1:2], before[0:E, 1:E + 1], nt_rep[:, 0:1], start=True, stop=True)
            pe.matmul(bank[1][:, 64:65 + E], nt_rep[:], before[0:E, 0:E + 1], start=True, stop=True).then_inc(base_ps, 1)
            pe.wait_ge(endge_done, 1)
            pe.matmul(bank[2][:, 0:TABLE], ones16[0:E - 1, :], end_ge[0:E - 1, :], start=True, stop=True).then_inc(etab_ps, 1)

            def sum_hits(n, buf, first, last):
                pe.wait_ge(hits_done, n + 1)
                for r in range(TOPK):
                    mm = pe.matmul(bank[3][:, 0:TABLE], hit_row[:, buf, r, :], hit_tile[:, buf, r, :],
                                   start=(first and r == 0), stop=(last and r == TOPK - 1), skip_group_check=True)
                mm.then_inc(hits_used, 1)

            sum_hits(0, 0, True, False)
            sum_hits(1, 1, False, False)
            with pe.Fori(1, NT // 2) as g:
                for u in range(2):
                    sum_hits(2 * g + u, u, False, False)
            pe.wait_ge(hits_used, NT)
            pe.sem_inc(table_ps, 1)

            def transpose_x(i, buf, arrived):
                pe.wait_ge(gath_in[buf], arrived)
                for c in range(KC):
                    mm = pe.transpose(bank[buf][:, c * P:(c + 1) * P], gath[:, buf, c * P:(c + 1) * P], ident[:])
                mm.then_inc(slotx_ps, 1)

            def expert_of(i):
                e = pe.value_load(expert_i[0:1, bass.ds(i, 1)], min_val=0, max_val=E - 1)
                return e

            def up(i, buf, e):
                pe.wait_ge(w_loaded, 32 * e + 32)
                pe.wait_ge(slotx_done, i + 1)
                for c in range(KC):
                    mm = pe.matmul(bank[2 + buf][:, 0:2 * F], xT[:, buf, c, :],
                                   wup[:, bass.ds(e % W_BUFS, 1), c * 2 * F:(c + 1) * 2 * F],
                                   start=(c == 0), stop=(c == KC - 1))
                mm.then_inc(gu_ps, 1)

            pe.wait_ge(table_done, 1)
            pe.wait_ge(regs_done, 3)
            pe.sem_inc(y_ps, 1)
            transpose_x(0, 0, 16)
            transpose_x(1, 1, 16)
            up(0, 0, expert_of(0))
            pairs = pe.value_load(pairs_i[0:1, 1:2], min_val=1, max_val=PAIRS)
            with pe.Fori(0, PAIRS) as g:
                with pe.If(g < pairs):
                    e_this = expert_of(2 * g)
                    for u in range(2):
                        i = 2 * g + u
                        e_next = expert_of(i + 1)
                        pe.wait_ge(hid_done, i + 1)
                        up(i + 1, 1 - u, e_next)
                        for c in range(FC):
                            mm = pe.transpose(bank[4][0:FP, c * P:(c + 1) * P],
                                              hid[:, u, c * FP:(c + 1) * FP], ident[:])
                        mm.then_inc(hidT_ps, 1)
                        transpose_x(i + 2, u, 16 * (g + 2))
                        pe.wait_ge(hidT_done, i + 1)
                        pe.wait_ge(ybank_free, i + 1)
                        for c in range(FC):
                            mm = pe.matmul(bank[5 + u][:], hidT[:, u, c, :],
                                           wdn[:, bass.ds(e_this % W_BUFS, 1), c * D:(c + 1) * D],
                                           start=(c == 0), stop=(c == FC - 1))
                        mm.then_inc(y_ps, 1)
                        e_this = e_next




def kernel(x, ctx_512, g_xattn, g_ffn, L0_xattn_W, L0_xattn_b, L0_ffn_gate_weight, L0_ffn_gate_up_proj,
           L0_ffn_down_proj, L0_ffn_similarity):
    import concourse.bacc as bacc
    from concourse.bass_utils import run_bass_kernel_spmd

    nc = bacc.Bacc("TRN2", target_bir_lowering=False, num_devices=1)
    B, N, D = x.shape
    E, F2, _ = L0_ffn_gate_up_proj.shape
    F = F2 // 2
    lay = np.ascontiguousarray
    up = np.asarray(L0_ffn_gate_up_proj).reshape(E, F2, D // P, P).transpose(0, 3, 2, 1).reshape(E, P, D // P * F2)
    down = np.asarray(L0_ffn_down_proj).reshape(E, D, 2, F // 2).transpose(0, 3, 2, 1).reshape(E, F // 2, 2 * D)
    arrays = {
        "x": lay(x),
        "ctxT": lay(np.asarray(ctx_512).transpose(0, 2, 1)),
        "W": lay(np.asarray(L0_xattn_W).reshape(2, -1).T),
        "b": lay(np.asarray(L0_xattn_b).reshape(1, 1)),
        "g_xattn": lay(np.asarray(g_xattn).reshape(1, 1)),
        "g_ffn": lay(np.asarray(g_ffn).reshape(1, 1)),
        "gwT": lay(np.asarray(L0_ffn_gate_weight).T),
        "wupT": lay(up),
        "wdnT": lay(down),
        "sim": lay(L0_ffn_similarity),
    }
    args = [nc.dram_tensor(k, list(a.shape), mybir.dt.from_np(a.dtype), kind="ExternalInput").ap()
            for k, a in arrays.items()]
    out = nc.dram_tensor("out", [B * N + P, D], F32, kind="ExternalOutput").ap()
    build(nc, *args, out)
    r = run_bass_kernel_spmd(nc, [arrays], core_ids=[0])
    return r.results[0]["out"][:B * N].reshape(B, N, D)
```

```python
from contextlib import ExitStack, contextmanager

import numpy as np
import concourse.bass as bass
from concourse import mybir

ALU = mybir.AluOpType
ACT = mybir.ActivationFunctionType
AX = mybir.AxisListType
F32 = mybir.dt.float32
F16 = mybir.dt.float16
I32 = mybir.dt.int32
U32 = mybir.dt.uint32

P = 128
TOPK = 8
PRIM = 4
THRESHOLD = 0.5
P_ASEM = 0.6
EPS = 1e-5
GROUP = 8
ACT_RANKS = 5
W_BUFS = 4


def build(nc, x, ctxT, W, b, g_xattn, g_ffn, gwT, wupT, wdnT, sim, out):
    B, N, D = x.shape
    DC = ctxT.shape[1]
    E = gwT.shape[1]
    F = wupT.shape[2] * P // (2 * D)
    KC = D // P
    FC = 2
    FP = F // FC
    TB = N // P
    TOK = B * N
    NT = TOK // P
    TILES = (TOK * TOPK + E * (P - 1)) // P
    PAIRS = (TILES + 1) // 2
    TABLE = 2 * PAIRS + 4
    ROW = D + E
    assert DC == P and D % P == 0 and FP <= P and PRIM * E == P and E == 32 and W_BUFS == 4 and PAIRS % GROUP == 0

    x_v = x.rearrange("b (t p) d -> b p t d", p=P)
    out_v = out.rearrange("(t p) d -> p t d", p=P)
    scratch = nc.dram_tensor("token_rows", [TOK + P, ROW], F32, kind="Internal").ap()
    scratch_v = scratch.rearrange("(t p) d -> p t d", p=P)

    with ExitStack() as ctx:
        def sb(name, shape, dt=F32):
            return ctx.enter_context(nc.sbuf_tensor(name, shape, dt))

        def ps(name, shape, dt=F32):
            return ctx.enter_context(nc.psum_tensor(name, shape, dt))

        def sem(name):
            return ctx.enter_context(nc.semaphore(name))

        ident = sb("ident", [P, P])
        ones = sb("ones", [P, P])
        ones16 = sb("ones16", [P, P], F16)
        before = sb("before", [P, P], F16)
        iota_e = sb("iota_e", [P, E])
        iota_tile = sb("iota_tile", [P, TABLE])
        iota16 = sb("iota16", [P, TABLE], F16)
        token_id1 = sb("token_id1", [P, NT])
        pad_id1 = sb("pad_id1", [P, 1])
        prim_order = sb("prim_order", [P, PRIM])
        gates = sb("gates", [1, 3])
        w_ij = sb("w_ij", [P, 2])
        ctx_sb = sb("ctx_sb", [P, B, N])
        gw_sb = sb("gw_sb", [P, KC, E])
        sim_bd = sb("sim_bd", [P, P])
        xs = sb("xs", [P, NT, D])
        wj_rep = sb("wj_rep", [P, P])
        gate_col = sb("gate_col", [P, 3])
        c_sig = sb("c_sig", [P, 1])
        c_ln = sb("c_ln", [P, 1])
        c_lnn = sb("c_lnn", [P, 1])
        si_b = sb("si_b", [P, NT])
        sig = sb("sig", [P, NT, N])
        eps_col = sb("eps_col", [P, 1])
        stats = sb("stats", [P, 2, NT, 6])
        mv = sb("mv", [P, 2, NT, 2])
        std = sb("std", [P, 2, NT])
        rstd = sb("rstd", [P, 2, NT])
        ln_a = sb("ln_a", [P, NT])
        ln_b = sb("ln_b", [P, NT])
        ln2_b = sb("ln2_b", [P, NT])
        rows_sb = sb("rows_sb", [P, NT, ROW])
        xnT = sb("xnT", [P, 2, D])
        rmax = sb("rmax", [P, NT])
        ctx_free = ctx_sb[:].rearrange("p b n -> p (b n)")
        probs = ctx_free[:, 0:NT * E].rearrange("p (t e) -> p t e", e=E)
        exps = ctx_free[:, NT * E:2 * NT * E].rearrange("p (t e) -> p t e", e=E)
        rsum = sb("rsum", [P, NT])
        rrec = sb("rrec", [P, NT])
        top = sb("top", [P, NT, TOPK])
        topi = sb("topi", [P, NT, TOPK], U32)
        topf = sb("topf", [P, NT, TOPK])
        oh = sb("oh", [P, NT, TOPK, E])
        wts = sb("wts", [P, NT, TOPK])
        wfin = sb("wfin", [P, NT, TOPK])
        ohT = sb("ohT", [P, 2, TB * P])
        cmul = ctx_free[:, 0:TB * PRIM * PRIM * E].rearrange(
            "p (t c e) -> p t c e", c=PRIM * PRIM, e=E)
        cand = sb("cand", [P, NT * PRIM, PRIM])
        best = sb("best", [P, NT * PRIM])
        eqb = sb("eqb", [P, NT * PRIM, PRIM])
        eqm = sb("eqm", [P, NT * PRIM])
        wgo = sb("wgo", [P, NT, PRIM])
        wadd = sb("wadd", [P, NT, PRIM])
        comb = sb("comb", [P, NT, E])
        mask = sb("mask", [P, NT, E], F16)
        cnt_i = sb("cnt_i", [E, 1], I32)
        nt_i = sb("nt_i", [E, 1], I32)
        nt_f = sb("nt_f", [E, 1])
        nt_rep = sb("nt_rep", [E, P], F16)
        base128 = sb("base128", [P, E])
        end_col = sb("end_col", [E, 1])
        end_ge = sb("end_ge", [E, TABLE], F16)
        expert_tab = sb("expert_tab", [P, TABLE])
        expert_i = sb("expert_i", [1, TABLE], I32)
        end_i = sb("end_i", [1, E], I32)
        pairs_i = sb("pairs_i", [1, 2], I32)
        slot_e = sb("slot_e", [P, NT, E])
        free = sig[:].rearrange("p t n -> p (t n)")
        used = [0]

        def reuse(*shape):
            size = int(np.prod(shape))
            part = free[:, used[0]:used[0] + size]
            used[0] += size
            names = "abc"[:len(shape)]
            return part.rearrange(f"p ({' '.join(names)}) -> p {' '.join(names)}", **dict(zip(names[1:], shape[1:])))

        slot_m = reuse(NT, TOPK, E)
        ohw = slot_m
        slot_r = sb("slot_r", [P, NT * TOPK])
        slot_i = sb("slot_i", [P, NT * TOPK], I32)
        srow_i = sb("srow_i", [P, NT * TOPK], I32)
        stile_i = sb("stile_i", [P, NT * TOPK], I32)
        srow = sb("srow", [P, NT * TOPK])
        stile = sb("stile", [P, NT * TOPK])
        valid = sb("valid", [P, NT * TOPK])
        srow_neg = sb("srow_neg", [P, NT * TOPK])
        away = sb("away", [P, ACT_RANKS, P], F16)
        hit_row = xnT[:].rearrange("p b d -> p (b d)").bitcast(F16)[:, 0:2 * TOPK * P].rearrange(
            "p (b r n) -> p b r n", b=2, r=TOPK)
        hit_tile = sb("hit_tile", [P, 2, TOPK, TABLE], F16)
        tab_f = sb("tab_f", [P, TABLE])
        token_tab = sb("token_tab", [P, TABLE], I32)
        wup = sb("wup", [P, W_BUFS, KC * 2 * F])
        wdn = sb("wdn", [FP, W_BUFS, FC * D])
        g_idx = sb("g_idx", [P, 2], I32)
        s_idx = sb("s_idx", [P, 2], I32)
        gath = reuse(2, ROW)
        xT = reuse(2, KC, P)
        wsel = sb("wsel", [P, E])
        slot_w = sb("slot_w", [P, 2])
        silu_g = reuse(2, F)
        hid = reuse(2, F)
        hidT = sb("hidT", [FP, 2, FC, P])
        ysb = reuse(2, D)
        zrow = sb("zrow", [P, ROW])
        turn = sb("turn", [1, 1])

        bank = [ps(f"bank{i}", [P, 512]) for i in range(8)]

        inputs_in = sem("inputs_in")
        router_in = sem("router_in")
        x_in = [sem(f"x_in{i}") for i in range(B)]
        consts = sem("consts")
        cfix = sem("cfix")
        gates_ps = sem("gates_ps")
        tanh_done = sem("tanh_done")
        bcol_done = sem("bcol_done")
        wjrep_done = sem("wjrep_done")
        si_ps = sem("si_ps")
        sib_done = sem("sib_done")
        sj_ps = sem("sj_ps")
        sig_done = sem("sig_done")
        var_done = sem("var_done")
        std_done = sem("std_done")
        lnab_done = sem("lnab_done")
        t1_done = sem("t1_done")
        x1_done = sem("x1_done")
        ln2_done = sem("ln2_done")
        xn_done = sem("xn_done")
        xnT_ps = sem("xnT_ps")
        xnT_done = sem("xnT_done")
        logit_ps = sem("logit_ps")
        shift_done = sem("shift_done")
        exp_done = sem("exp_done")
        oh_done = sem("oh_done")
        ohT_ps = sem("ohT_ps")
        ohT_done = sem("ohT_done")
        simrow_ps = sem("simrow_ps")
        simrow_used = sem("simrow_used")
        mask_done = sem("mask_done")
        combrow_done = sem("combrow_done")
        pos_ps = sem("pos_ps")
        ntrep_done = sem("ntrep_done")
        base_ps = sem("base_ps")
        endge_done = sem("endge_done")
        etab_ps = sem("etab_ps")
        regs_done = sem("regs_done")
        srow_done = sem("srow_done")
        hits_done = sem("hits_done")
        rowhits_done = sem("rowhits_done")
        away_done = sem("away_done")
        hits_used = sem("hits_used")
        table_ps = sem("table_ps")
        table_done = sem("table_done")
        chain = sem("chain")
        x1_stored = sem("x1_stored")
        rows_stored = sem("rows_stored")
        w_loaded = sem("w_loaded")
        out_added = sem("out_added")
        idx_staged = sem("idx_staged")
        sidx_staged = sem("sidx_staged")
        gath_in = [sem("gath_in0"), sem("gath_in1")]
        slotx_ps = sem("slotx_ps")
        slotx_done = sem("slotx_done")
        gu_ps = sem("gu_ps")
        silu_done = sem("silu_done")
        hid_done = sem("hid_done")
        hidT_ps = sem("hidT_ps")
        hidT_done = sem("hidT_done")
        y_ps = sem("y_ps")
        ybank_free = sem("ybank_free")
        y_done = sem("y_done")
        wsel_done = sem("wsel_done")
        slotw_done = sem("slotw_done")

        block = ctx.enter_context(nc.Block())

        @contextmanager
        def slot_pairs(engine, pairs):
            with engine.Fori(0, PAIRS // GROUP) as group:
                with engine.If(group * GROUP < pairs):
                    with engine.Fori(0, GROUP) as k:
                        with engine.If(group * GROUP + k < pairs):
                            yield group * GROUP + k

        def load_expert(sp, e, buf):
            sp.dma_start(wup[:, buf, :], wupT[e]).then_inc(w_loaded, 16)
            sp.dma_start(wdn[:, buf, :], wdnT[e]).then_inc(w_loaded, 16)

        @block.sync
        def _(sp):
            sp.dma_start(gates[:, 0:1], b).then_inc(inputs_in, 16)
            sp.dma_start(gates[:, 1:2], g_xattn).then_inc(inputs_in, 16)
            sp.dma_start(gates[:, 2:3], g_ffn).then_inc(inputs_in, 16)
            sp.dma_start(w_ij[:], W).then_inc(inputs_in, 16)
            sp.dma_start(ctx_sb[:], ctxT.rearrange("b d n -> d b n")).then_inc(inputs_in, 16)
            for q in range(B):
                sp.dma_start(xs[:, q * TB:(q + 1) * TB, :], x_v[q]).then_inc(x_in[q], 16)
                if q == 0:
                    sp.dma_start(gw_sb[:], gwT.rearrange("(c p) e -> p c e", p=P)).then_inc(router_in, 16)
                    sp.wait_ge(consts, 1)
                    for k in range(PRIM):
                        sp.dma_start(sim_bd[E * k:E * (k + 1), E * k:E * (k + 1)], sim).then_inc(router_in, 16)
            for e in range(W_BUFS):
                load_expert(sp, e, e)
                sp.wait_ge(w_loaded, 32 * (e + 1))
                if e < B:
                    sp.wait_ge(x1_done, TB * (e + 1))
                    sp.dma_start(out_v[:, e * TB:(e + 1) * TB, :], xs[:, e * TB:(e + 1) * TB, :]).then_inc(x1_stored, 16)
            sp.wait_ge(combrow_done, 1)
            sp.dma_start(scratch_v[:, 0:NT, :], rows_sb[:]).then_inc(rows_stored, 16)
            sp.wait_ge(regs_done, 3)
            with sp.Fori(1, E // W_BUFS) as k:
                for j in range(W_BUFS):
                    end = sp.value_load(end_i[0:1, bass.ds(W_BUFS * (k - 1) + j, 1)], min_val=0, max_val=TILES)
                    sp.wait_ge(y_ps, end + 1)
                    sp.wait_ge(w_loaded, 32 * (W_BUFS * k + j))
                    load_expert(sp, W_BUFS * k + j, j)
            sp.wait_ge(w_loaded, 32 * E)

        @block.gpsimd
        def _(pool):
            pool.memset(sim_bd[:], 0.0).then_inc(consts, 1)
            pool.memset(ident[:], 0.0).then_inc(cfix, 1)
            pool.memset(before[:], 1.0).then_inc(cfix, 1)
            pool.memset(ones[:], 1.0).then_inc(consts, 1)
            pool.memset(ones16[:], 1.0).then_inc(consts, 1)
            pool.wait_ge(cfix, 2)
            pool.affine_select(out=ident[:], in_=ident[:], compare_op=ALU.not_equal, fill=1.0, base=0,
                               pattern=[[-1, P]], channel_multiplier=1).then_inc(consts, 1)
            pool.affine_select(out=before[:], in_=before[:], compare_op=ALU.is_gt, fill=0.0, base=0,
                               pattern=[[1, P]], channel_multiplier=-1).then_inc(consts, 1)
            exact = dict(allow_small_or_imprecise_dtypes=True)
            pool.iota(iota_e[:], [[1, E]], 0, 0, **exact).then_inc(consts, 1)
            pool.iota(iota_tile[:], [[1, TABLE]], 0, 0, **exact).then_inc(consts, 1)
            pool.iota(iota16[:], [[1, TABLE]], 0, 0, **exact).then_inc(consts, 1)
            pool.iota(token_id1[:], [[P, NT]], 1, 1, **exact).then_inc(consts, 1)
            pool.iota(pad_id1[:], [[0, 1]], TOK + 1, 1, **exact).then_inc(consts, 1)
            pool.iota(prim_order[:], [[-1, PRIM]], PRIM, 0, **exact).then_inc(consts, 1)
            pool.memset(zrow[:], 0.0).then_inc(consts, 1)
            pool.memset(eps_col[:], EPS).then_inc(consts, 1)
            pool.wait_ge(router_in, 16 * (1 + PRIM))
            pool.affine_select(out=sim_bd[:], in_=sim_bd[:], compare_op=ALU.not_equal, fill=1.0, base=0,
                               pattern=[[-1, P]], channel_multiplier=1).then_inc(consts, 1)
            pool.wait_ge(consts, 13)
            pool.dma_start(scratch_v[:, NT, :], zrow[:]).then_inc(out_added, 16)
            pool.dma_start(out_v[:, NT, :], zrow[:, 0:D]).then_inc(out_added, 16)

            def settle():
                pool.tensor_tensor(turn[:], zrow[0:1, 0:1], zrow[0:1, 0:1], ALU.add)

            def gather(i, buf):
                pool.tensor_copy(g_idx[:, buf:buf + 1], token_tab[:, bass.ds(i, 1)]).then_inc(idx_staged, 1)
                pool.wait_ge(idx_staged, i + 1)
                settle()
                pool.indirect_dma_start(
                    out=gath[:, buf, :], out_offset=None, in_=scratch,
                    in_offset=bass.IndirectOffsetOnAxis(ap=g_idx[:, buf:buf + 1], axis=0),
                ).then_inc(gath_in[buf], 16)

            pool.wait_ge(table_done, 1)
            pool.wait_ge(rows_stored, 16)
            pool.wait_ge(x1_stored, 16 * B)
            pool.wait_ge(out_added, 32)
            gather(0, 0)
            gather(1, 1)
            pool.wait_ge(slotx_ps, 1)
            pool.wait_ge(slotw_done, 1)
            pool.wait_ge(gath_in[0], 16)
            gather(2, 0)
            pairs = pool.value_load(pairs_i[0:1, 1:2], min_val=1, max_val=PAIRS)
            with slot_pairs(pool, pairs) as g:
                    for u in range(2):
                        i = 2 * g + u
                        pool.wait_ge(slotx_ps, i + 2)
                        pool.wait_ge(slotw_done, i + 2)
                        pool.wait_ge(gath_in[1 - u], 16 * (g + 1 + u))
                        gather(i + 3, 1 - u)
                        pool.wait_ge(out_added, 16 * (i + 2))
                        pool.tensor_copy(s_idx[:, u:u + 1], token_tab[:, bass.ds(i, 1)]).then_inc(sidx_staged, 1)
                        pool.wait_ge(sidx_staged, i + 1)
                        pool.wait_ge(y_done, i + 1)
                        settle()
                        pool.indirect_dma_start(
                            out=out, out_offset=bass.IndirectOffsetOnAxis(ap=s_idx[:, u:u + 1], axis=0),
                            in_=ysb[:, u, :], in_offset=None, compute_op=ALU.add,
                        ).then_inc(out_added, 16)
            pool.wait_ge(out_added, 32 * pairs + 32)
            pool.wait_ge(gath_in[0], 16 * pairs + 32)
            pool.wait_ge(gath_in[1], 16 * pairs + 16)

        @block.scalar
        def _(act):
            act.wait_ge(gates_ps, 1)
            act.activation(gate_col[:, 1:3], bank[0][:, 1:3], ACT.Tanh).then_inc(tanh_done, 1)
            act.wait_ge(sib_done, 1)
            for q in range(B):
                act.wait_ge(sj_ps, q + 1)
                for t in range(TB):
                    n = q * TB + t
                    act.activation(sig[:, n, :], bank[2 + q % 2][:], ACT.Sigmoid,
                                   bias=si_b[:, n:n + 1]).then_inc(sig_done, 1)

            def add_norm(q):
                for n in range(q * TB, (q + 1) * TB):
                    act.activation(xs[:, n, :], xs[:, n, :], ACT.Identity, bias=ln_b[:, n:n + 1],
                                   scale=ln_a[:, n:n + 1]).then_inc(t1_done, 1)

            act.wait_ge(consts, 14)
            act.wait_ge(var_done, 1)
            act.activation(std[:, 0, :], mv[:, 0, :, 1], ACT.Sqrt, bias=eps_col[:]).then_inc(std_done, 1)
            act.wait_ge(lnab_done, 1)
            add_norm(0)
            for q in range(B):
                if q + 1 < B:
                    add_norm(q + 1)
                act.wait_ge(var_done, q + 2)
                act.activation(std[:, 1, q * TB:(q + 1) * TB], mv[:, 1, q * TB:(q + 1) * TB, 1], ACT.Sqrt,
                               bias=eps_col[:]).then_inc(std_done, 1)
                act.wait_ge(ln2_done, q + 1)
                for n in range(q * TB, (q + 1) * TB):
                    act.activation(rows_sb[:, n, 0:D], xs[:, n, :], ACT.Identity, bias=ln2_b[:, n:n + 1],
                                   scale=rstd[:, 1, n:n + 1]).then_inc(xn_done, 1)
                for n in range(q * TB, (q + 1) * TB):
                    act.wait_ge(xnT_ps, n + 1)
                    if n >= 2:
                        act.wait_ge(logit_ps, n - 1)
                    act.activation(xnT[:, n % 2, :], bank[4 + n % 2][:], ACT.Copy).then_inc(xnT_done, 1)
            act.wait_ge(shift_done, B)
            act.activation(exps, probs, ACT.Exp).then_inc(exp_done, 1)
            for q in range(B):
                act.wait_ge(ohT_ps, q + 1)
                if q >= 2:
                    act.wait_ge(simrow_ps, q - 1)
                act.activation(ohT[:, q % 2, :], bank[4 + q % 2][:], ACT.Copy).then_inc(ohT_done, 1)

            def row_hits(n, buf):
                for r in range(ACT_RANKS):
                    ins = act.activation(away[:, r, :], iota16[:, 0:P], ACT.Abs,
                                         bias=srow_neg[:, bass.ds(n * TOPK + r, 1)])
                ins.then_inc(away_done, 1)
                act.wait_ge(away_done, n + 1)
                act.activation(hit_row[:, buf, 0:ACT_RANKS, :], away[:], ACT.Relu, bias=1.0,
                               scale=-1.0).then_inc(rowhits_done, 1)

            act.wait_ge(srow_done, 1)
            row_hits(0, 0)
            act.wait_ge(rowhits_done, 1)
            row_hits(1, 1)
            with act.Fori(1, NT // 2) as g:
                for u in range(2):
                    act.wait_ge(hits_used, 2 * g + u - 1)
                    act.wait_ge(rowhits_done, 2 * g + u)
                    row_hits(2 * g + u, u)

            def evacuate_x(i, buf):
                act.wait_ge(slotx_ps, i + 1)
                act.activation(xT[:, buf].rearrange("p c n -> p (c n)"), bank[buf][:],
                               ACT.Copy).then_inc(slotx_done, 1)

            def silu(i, buf):
                act.wait_ge(gu_ps, i + 1)
                act.activation(silu_g[:, buf, :], bank[2 + buf][:, 0:F], ACT.Silu).then_inc(silu_done, 1)

            evacuate_x(0, 0)
            evacuate_x(1, 1)
            silu(0, 0)
            act.wait_ge(regs_done, 3)
            pairs = act.value_load(pairs_i[0:1, 1:2], min_val=1, max_val=PAIRS)
            with slot_pairs(act, pairs) as g:
                    for u in range(2):
                        i = 2 * g + u
                        act.wait_ge(hid_done, i + 1)
                        silu(i + 1, 1 - u)
                        evacuate_x(i + 2, u)

        @block.vector
        def _(dve):
            steps = [0]

            def after(ins):
                steps[0] += 1
                ins.then_inc(chain, 1)
                dve.wait_ge(chain, steps[0])

            dve.wait_ge(consts, 2)
            dve.wait_ge(inputs_in, 16 * 5)
            dve.tensor_scalar(wj_rep[:], ones[:], w_ij[:, 1:2], None, ALU.mult).then_inc(wjrep_done, 1)
            dve.wait_ge(tanh_done, 1)
            dve.tensor_copy(gate_col[:, 0:1], bank[0][:, 0:1]).then_inc(bcol_done, 1)
            dve.wait_ge(bcol_done, 1)
            dve.wait_ge(si_ps, 1)
            dve.tensor_scalar(si_b[:], bank[1][:, 0:NT], gate_col[:, 0:1], None, ALU.add).then_inc(sib_done, 1)
            dve.wait_ge(tanh_done, 1)
            dve.tensor_scalar(c_sig[:], gate_col[:, 1:2], P_ASEM, None, ALU.mult)
            dve.tensor_scalar(c_ln[:], gate_col[:, 1:2], 1.0 - P_ASEM, None, ALU.mult)
            after(dve.tensor_scalar(c_lnn[:], gate_col[:, 1:2], P_ASEM - 1.0, None, ALU.mult))
            dve.wait_ge(consts, 14)

            def moments(which, tiles, signals):
                for n in tiles:
                    if which == 0 and n % TB == 0:
                        dve.wait_ge(x_in[n // TB], 16)
                    ins = dve.bn_stats(stats[:, which, n, :], xs[:, n, :])
                after(ins)
                for n in tiles:
                    ins = dve.bn_aggr(mv[:, which, n, :], stats[:, which, n, :])
                ins.then_inc(var_done, 1)
                dve.wait_ge(std_done, signals)
                after(dve.reciprocal(rstd[:, which, tiles[0]:tiles[-1] + 1], std[:, which, tiles[0]:tiles[-1] + 1]))

            moments(0, range(NT), 1)
            after(dve.tensor_scalar(ln_a[:], rstd[:, 0, :], c_ln[:], 1.0, ALU.mult, ALU.add))
            dve.scalar_tensor_tensor(out=ln_b[:], in0=mv[:, 0, :, 0], scalar=c_lnn[:],
                                     in1=rstd[:, 0, :], op0=ALU.mult, op1=ALU.mult).then_inc(lnab_done, 1)
            for q in range(B):
                n0, n1 = q * TB, (q + 1) * TB
                for n in range(n0, n1):
                    dve.wait_ge(t1_done, n + 1)
                    dve.wait_ge(sig_done, n + 1)
                    dve.scalar_tensor_tensor(out=xs[:, n, :], in0=sig[:, n, :], scalar=c_sig[:], in1=xs[:, n, :],
                                             op0=ALU.mult, op1=ALU.add).then_inc(x1_done, 1)
                dve.wait_ge(x1_done, n1)
                moments(1, range(n0, n1), q + 2)
                dve.scalar_tensor_tensor(out=ln2_b[:, n0:n1], in0=mv[:, 1, n0:n1, 0], scalar=-1.0,
                                         in1=rstd[:, 1, n0:n1], op0=ALU.mult, op1=ALU.mult).then_inc(ln2_done, 1)

            def spread(v, n):
                return v.unsqueeze(2).broadcast_to([v.shape[0], v.shape[1], n])

            dve.wait_ge(logit_ps, NT)
            for q in range(B):
                ins = dve.tensor_reduce(rmax[:, q * TB:(q + 1) * TB],
                                        bank[q][:, 0:TB * E].rearrange("p (t e) -> p t e", e=E), AX.X, ALU.max)
            after(ins)
            for q in range(B):
                dve.tensor_tensor(probs[:, q * TB:(q + 1) * TB], bank[q][:, 0:TB * E].rearrange("p (t e) -> p t e", e=E),
                                  spread(rmax[:, q * TB:(q + 1) * TB], E), ALU.subtract).then_inc(shift_done, 1)
            dve.wait_ge(exp_done, 1)
            after(dve.tensor_reduce(rsum[:], exps, AX.X, ALU.add))
            after(dve.reciprocal(rrec[:], rsum[:]))
            after(dve.tensor_tensor(probs, exps, spread(rrec[:], E), ALU.mult))
            for n in range(NT):
                ins = dve.max(top[:, n, :], probs[:, n, :])
            after(ins)
            for n in range(NT):
                ins = dve.max_index(topi[:, n, :], top[:, n, :], probs[:, n, :])
            after(ins)
            after(dve.tensor_copy(topf[:], topi[:]))
            for q in range(B):
                n0, n1 = q * TB, (q + 1) * TB
                dve.tensor_tensor(oh[:, n0:n1].rearrange("p t r e -> p (t r) e"),
                                  spread(topf[:, n0:n1].rearrange("p t r -> p (t r)"), E),
                                  iota_e[:].unsqueeze(1).broadcast_to([P, TB * TOPK, E]),
                                  ALU.is_equal).then_inc(oh_done, 1)
            after(dve.tensor_reduce(rsum[:], top[:], AX.X, ALU.add))
            after(dve.tensor_scalar(rsum[:], rsum[:], 1e-12, None, ALU.max))
            after(dve.reciprocal(rrec[:], rsum[:]))
            dve.tensor_tensor(wts[:], top[:], spread(rrec[:], TOPK), ALU.mult)
            for q in range(B):
                dve.wait_ge(simrow_ps, q + 1)
                for t in range(TB):
                    rows = bank[6 + q % 2][:, t * P:(t + 1) * P].rearrange("p (k e) -> p k e", e=E)
                    rows = rows.unsqueeze(2).broadcast_to([P, PRIM, PRIM, E])
                    prim = oh[:, q * TB + t, 0:PRIM, :].unsqueeze(1).broadcast_to([P, PRIM, PRIM, E])
                    ins = dve.tensor_tensor(cmul[:, t].rearrange("p (k j) e -> p k j e", j=PRIM), rows, prim, ALU.mult)
                ins.then_inc(simrow_used, 1)
                dve.wait_ge(simrow_used, q + 1)
                after(dve.tensor_reduce(cand[:, q * TB * PRIM:(q + 1) * TB * PRIM].rearrange("p k j -> p (k j)"),
                                        cmul.rearrange("p t c e -> p (t c) e"), AX.X, ALU.add))
            after(dve.tensor_reduce(best[:], cand[:], AX.X, ALU.max))
            after(dve.tensor_tensor(eqb[:], cand[:], spread(best[:], PRIM), ALU.is_equal))
            after(dve.tensor_tensor(eqb[:], eqb[:], prim_order[:].unsqueeze(1).broadcast_to([P, NT * PRIM, PRIM]),
                                    ALU.mult))
            after(dve.tensor_reduce(eqm[:], eqb[:], AX.X, ALU.max))
            after(dve.tensor_tensor(eqb[:], eqb[:], spread(eqm[:], PRIM), ALU.is_equal))
            best_t = best[:].rearrange("p (t k) -> p t k", k=PRIM)
            dve.scalar_tensor_tensor(out=wfin[:, :, PRIM:], in0=best_t, scalar=THRESHOLD,
                                     in1=wts[:, :, PRIM:], op0=ALU.is_lt, op1=ALU.mult)
            after(dve.scalar_tensor_tensor(out=wgo[:], in0=best_t, scalar=THRESHOLD, in1=wts[:, :, PRIM:],
                                           op0=ALU.is_ge, op1=ALU.mult))
            after(dve.tensor_tensor(eqb[:], eqb[:], spread(wgo[:].rearrange("p t k -> p (t k)"), PRIM), ALU.mult))
            after(dve.tensor_reduce(wadd[:], eqb[:].rearrange("p (t k) j -> p t j k", k=PRIM), AX.X, ALU.add))
            after(dve.tensor_tensor(wfin[:, :, 0:PRIM], wts[:, :, 0:PRIM], wadd[:], ALU.add))
            after(dve.tensor_tensor(ohw.rearrange("p t r e -> p (t r) e"), oh[:].rearrange("p t r e -> p (t r) e"),
                                    spread(wfin[:].rearrange("p t r -> p (t r)"), E), ALU.mult))
            after(dve.tensor_reduce(comb[:], ohw.rearrange("p t r e -> p t e r"), AX.X, ALU.add))
            dve.tensor_scalar(mask[:], comb[:], 0.0, None, ALU.is_gt).then_inc(mask_done, 1)
            dve.wait_ge(xn_done, NT)
            dve.tensor_scalar(rows_sb[:, :, D:], comb[:], gate_col[:, 2:3], None, ALU.mult).then_inc(combrow_done, 1)

            dve.wait_ge(pos_ps, 1)
            after(dve.tensor_scalar(cnt_i[:], bank[1][0:E, 0:1], float(P - 1), None, ALU.add))
            after(dve.tensor_scalar(nt_i[:], cnt_i[:], 7, None, ALU.arith_shift_right))
            after(dve.tensor_copy(nt_f[:], nt_i[:]))
            dve.tensor_scalar(nt_rep[:], ones[0:E, :], nt_f[:], None, ALU.mult).then_inc(ntrep_done, 1)
            dve.wait_ge(base_ps, 1)
            dve.tensor_copy(end_col[:], bank[1][0:E, 1:2])
            dve.tensor_copy(end_i[:], bank[1][0:1, 65:65 + E]).then_inc(regs_done, 1)
            dve.tensor_scalar(pairs_i[:, 0:1], bank[1][0:1, 64 + E:65 + E], 1.0, None, ALU.add)
            after(dve.tensor_scalar(base128[:], bank[1][:, 64:64 + E], float(P), None, ALU.mult))
            dve.tensor_scalar(pairs_i[:, 1:2], pairs_i[:, 0:1], 1, None, ALU.arith_shift_right).then_inc(regs_done, 1)
            dve.tensor_scalar(end_ge[:], iota_tile[0:E, :], end_col[:], None, ALU.is_ge).then_inc(endge_done, 1)
            after(dve.tensor_tensor(slot_e[:], bank[0][:].rearrange("p (t e) -> p t e", e=E),
                                    base128[:].unsqueeze(1).broadcast_to([P, NT, E]), ALU.add))
            dve.tensor_scalar(valid[:], wfin[:].rearrange("p t r -> p (t r)"), 0.0, None, ALU.is_gt)
            for n in range(NT):
                ins = dve.tensor_tensor(slot_m[:, n], oh[:, n],
                                        slot_e[:, n].unsqueeze(1).broadcast_to([P, TOPK, E]), ALU.mult)
            after(ins)
            after(dve.tensor_reduce(slot_r[:], slot_m.rearrange("p t r e -> p (t r) e"), AX.X, ALU.add))
            after(dve.scalar_tensor_tensor(out=slot_r[:], in0=slot_r[:], scalar=1.0, in1=valid[:],
                                           op0=ALU.add, op1=ALU.mult))
            after(dve.tensor_scalar(slot_i[:], slot_r[:], -1.0, None, ALU.add))
            dve.tensor_scalar(srow_i[:], slot_i[:], P - 1, None, ALU.bitwise_and)
            after(dve.tensor_scalar(stile_i[:], slot_i[:], 7, None, ALU.arith_shift_right))
            dve.tensor_copy(srow[:], srow_i[:])
            dve.tensor_scalar(srow_neg[:], srow_i[:], -1.0, None, ALU.mult).then_inc(srow_done, 1)
            after(dve.tensor_copy(stile[:], stile_i[:]))
            dve.wait_ge(etab_ps, 1)
            dve.tensor_copy(expert_i[:], bank[2][0:1, 0:TABLE]).then_inc(regs_done, 1)
            dve.tensor_copy(expert_tab[:], bank[2][:, 0:TABLE])

            def hits(n, buf):
                for r in range(ACT_RANKS, TOPK):
                    dve.tensor_scalar(hit_row[:, buf, r, :], iota16[:, 0:P], srow[:, bass.ds(n * TOPK + r, 1)],
                                      None, ALU.is_equal)
                for r in range(TOPK):
                    ins = dve.tensor_scalar(hit_tile[:, buf, r, :], iota16[:],
                                            stile[:, bass.ds(n * TOPK + r, 1)], token_id1[:, bass.ds(n, 1)],
                                            ALU.is_equal, ALU.mult)
                ins.then_inc(hits_done, 1)

            hits(0, 0)
            hits(1, 1)
            with dve.Fori(1, NT // 2) as g:
                for u in range(2):
                    dve.wait_ge(hits_used, 2 * g + u - 1)
                    hits(2 * g + u, u)
            dve.wait_ge(table_ps, 1)
            after(dve.tensor_scalar(tab_f[:], bank[3][:, 0:TABLE], 0.0, pad_id1[:], ALU.is_equal, ALU.mult))
            dve.scalar_tensor_tensor(out=token_tab[:], in0=bank[3][:, 0:TABLE], scalar=-1.0, in1=tab_f[:],
                                     op0=ALU.add, op1=ALU.add).then_inc(table_done, 1)

            def weigh(i, buf, arrived):
                dve.wait_ge(gath_in[buf], arrived)
                if not isinstance(i, int):
                    dve.wait_ge(slotw_done, i)
                dve.scalar_tensor_tensor(out=wsel[:], in0=iota_e[:], scalar=expert_tab[:, bass.ds(i, 1)],
                                         in1=gath[:, buf, D:], op0=ALU.is_equal, op1=ALU.mult).then_inc(wsel_done, 1)
                dve.wait_ge(wsel_done, i + 1)
                dve.tensor_reduce(slot_w[:, buf:buf + 1], wsel[:], AX.X, ALU.add).then_inc(slotw_done, 1)

            def hidden(i, buf):
                dve.wait_ge(silu_done, i + 1)
                dve.tensor_tensor(hid[:, buf, :], silu_g[:, buf, :], bank[2 + buf][:, F:2 * F],
                                  ALU.mult).then_inc(hid_done, 1)

            weigh(0, 0, 16)
            hidden(0, 0)
            dve.sem_inc(ybank_free, 2)
            pairs = dve.value_load(pairs_i[0:1, 1:2], min_val=1, max_val=PAIRS)
            with slot_pairs(dve, pairs) as g:
                    for u in range(2):
                        i = 2 * g + u
                        weigh(i + 1, 1 - u, 16 * (g + 1 + u))
                        dve.wait_ge(hidT_ps, i + 1)
                        dve.tensor_copy(hidT[:, u].rearrange("p c n -> p (c n)"),
                                        bank[4][0:FP, 0:FC * P]).then_inc(hidT_done, 1)
                        hidden(i + 1, 1 - u)
                        dve.wait_ge(y_ps, i + 2)
                        dve.wait_ge(out_added, 16 * (i + 1))
                        dve.tensor_scalar(ysb[:, u, :], bank[5 + u][:], slot_w[:, u:u + 1], None,
                                          ALU.mult).then_inc(y_done, 1)
                        dve.wait_ge(y_done, i + 1)
                        dve.sem_inc(ybank_free, 1)

        @block.tensor
        def _(pe):
            pe.wait_ge(consts, 2)
            pe.wait_ge(inputs_in, 16 * 5)
            pe.matmul(bank[0][:, 0:3], ones[0:1, :], gates[:], start=True, stop=True).then_inc(gates_ps, 1)
            for n in range(NT):
                q, t = divmod(n, TB)
                mm = pe.matmul(bank[1][:, n:n + 1], ctx_sb[:, q, t * P:(t + 1) * P], w_ij[:, 0:1], start=True, stop=True)
            mm.then_inc(si_ps, 1)
            pe.wait_ge(wjrep_done, 1)
            for q in range(B):
                if q >= 2:
                    pe.wait_ge(sig_done, TB * (q - 1))
                pe.matmul(bank[2 + q % 2][:], wj_rep[:], ctx_sb[:, q, :], start=True, stop=True).then_inc(sj_ps, 1)
            pe.wait_ge(consts, 4)
            pe.wait_ge(router_in, 16 * (1 + PRIM))

            def turn_ranks(q):
                pe.wait_ge(oh_done, q + 1)
                if q >= 2:
                    pe.wait_ge(ohT_done, q - 1)
                for t in range(TB):
                    mm = pe.transpose(bank[4 + q % 2][:, t * P:(t + 1) * P],
                                      oh[:, q * TB + t, PRIM:, :].rearrange("p k e -> p (k e)"), ident[:])
                mm.then_inc(ohT_ps, 1)

            def similar(q):
                pe.wait_ge(ohT_done, q + 1)
                if q >= 2:
                    pe.wait_ge(simrow_used, q - 1)
                for t in range(TB):
                    mm = pe.matmul(bank[6 + q % 2][:, t * P:(t + 1) * P], ohT[:, q % 2, t * P:(t + 1) * P], sim_bd[:],
                                   start=True, stop=True)
                mm.then_inc(simrow_ps, 1)

            def xn_transpose(n):
                pe.wait_ge(xn_done, n + 1)
                if n >= 2:
                    pe.wait_ge(xnT_done, n - 1)
                for c in range(KC):
                    mm = pe.transpose(bank[4 + n % 2][:, c * P:(c + 1) * P], rows_sb[:, n, c * P:(c + 1) * P], ident[:])
                mm.then_inc(xnT_ps, 1)

            def logits(n):
                pe.wait_ge(xnT_done, n + 1)
                for c in range(KC):
                    mm = pe.matmul(bank[n // TB][:, n % TB * E:(n % TB + 1) * E], xnT[:, n % 2, c * P:(c + 1) * P], gw_sb[:, c, :],
                                   start=(c == 0), stop=(c == KC - 1))
                mm.then_inc(logit_ps, 1)

            for q in range(B):
                xn_transpose(q * TB)
                for t in range(TB):
                    n = q * TB + t
                    if t + 1 < TB:
                        xn_transpose(n + 1)
                    logits(n)
            pe.wait_ge(consts, 14)
            pe.wait_ge(xnT_done, NT)
            turn_ranks(0)
            for q in range(B):
                if q + 1 < B:
                    turn_ranks(q + 1)
                similar(q)

            pe.wait_ge(mask_done, 1)
            allm = mask[:].rearrange("p t e -> p (t e)")
            pe.matmul(bank[0][:], before[:], allm, start=True, stop=False, skip_group_check=True)
            for n in range(NT - 1):
                pe.matmul(bank[0][:, (n + 1) * E:].rearrange("p (t e) -> p t e", e=E), ones16[:],
                          mask[:, n, :].unsqueeze(1).broadcast_to([P, NT - 1 - n, E]),
                          start=False, stop=(n == NT - 2), skip_group_check=True)
            for n in range(NT):
                mm = pe.matmul(bank[1][0:E, 0:1], mask[:, n, :], ones16[:, 0:1], start=(n == 0), stop=(n == NT - 1))
            mm.then_inc(pos_ps, 1)
            pe.wait_ge(ntrep_done, 1)
            pe.matmul(bank[1][0:E, 1:2], before[0:E, 1:E + 1], nt_rep[:, 0:1], start=True, stop=True)
            pe.matmul(bank[1][:, 64:65 + E], nt_rep[:], before[0:E, 0:E + 1], start=True, stop=True).then_inc(base_ps, 1)
            pe.wait_ge(endge_done, 1)
            pe.matmul(bank[2][:, 0:TABLE], ones16[0:E - 1, :], end_ge[0:E - 1, :], start=True, stop=True).then_inc(etab_ps, 1)

            def sum_hits(n, buf, first, last):
                pe.wait_ge(hits_done, n + 1)
                pe.wait_ge(rowhits_done, n + 1)
                for r in range(TOPK):
                    mm = pe.matmul(bank[3][:, 0:TABLE], hit_row[:, buf, r, :], hit_tile[:, buf, r, :],
                                   start=(first and r == 0), stop=(last and r == TOPK - 1), skip_group_check=True)
                mm.then_inc(hits_used, 1)

            sum_hits(0, 0, True, False)
            sum_hits(1, 1, False, False)
            with pe.Fori(1, NT // 2) as g:
                for u in range(2):
                    sum_hits(2 * g + u, u, False, False)
            pe.wait_ge(hits_used, NT)
            pe.sem_inc(table_ps, 1)

            def transpose_x(i, buf, arrived):
                pe.wait_ge(gath_in[buf], arrived)
                for c in range(KC):
                    mm = pe.transpose(bank[buf][:, c * P:(c + 1) * P], gath[:, buf, c * P:(c + 1) * P], ident[:])
                mm.then_inc(slotx_ps, 1)

            def expert_of(i):
                e = pe.value_load(expert_i[0:1, bass.ds(i, 1)], min_val=0, max_val=E - 1)
                return e

            def up(i, buf, e):
                pe.wait_ge(w_loaded, 32 * e + 32)
                pe.wait_ge(slotx_done, i + 1)
                for c in range(KC):
                    mm = pe.matmul(bank[2 + buf][:, 0:2 * F], xT[:, buf, c, :],
                                   wup[:, bass.ds(e % W_BUFS, 1), c * 2 * F:(c + 1) * 2 * F],
                                   start=(c == 0), stop=(c == KC - 1))
                mm.then_inc(gu_ps, 1)

            pe.wait_ge(table_done, 1)
            pe.wait_ge(regs_done, 3)
            pe.sem_inc(y_ps, 1)
            transpose_x(0, 0, 16)
            transpose_x(1, 1, 16)
            up(0, 0, expert_of(0))
            pairs = pe.value_load(pairs_i[0:1, 1:2], min_val=1, max_val=PAIRS)
            with slot_pairs(pe, pairs) as g:
                    e_this = expert_of(2 * g)
                    for u in range(2):
                        i = 2 * g + u
                        e_next = expert_of(i + 1)
                        pe.wait_ge(hid_done, i + 1)
                        for c in range(FC):
                            mm = pe.transpose(bank[4][0:FP, c * P:(c + 1) * P],
                                              hid[:, u, c * FP:(c + 1) * FP], ident[:])
                        mm.then_inc(hidT_ps, 1)
                        up(i + 1, 1 - u, e_next)
                        transpose_x(i + 2, u, 16 * (g + 2))
                        pe.wait_ge(hidT_done, i + 1)
                        pe.wait_ge(ybank_free, i + 1)
                        for c in range(FC):
                            mm = pe.matmul(bank[5 + u][:], hidT[:, u, c, :],
                                           wdn[:, bass.ds(e_this % W_BUFS, 1), c * D:(c + 1) * D],
                                           start=(c == 0), stop=(c == FC - 1))
                        mm.then_inc(y_ps, 1)
                        e_this = e_next




def kernel(x, ctx_512, g_xattn, g_ffn, L0_xattn_W, L0_xattn_b, L0_ffn_gate_weight, L0_ffn_gate_up_proj,
           L0_ffn_down_proj, L0_ffn_similarity):
    import concourse.bacc as bacc
    from concourse.bass_utils import run_bass_kernel_spmd

    nc = bacc.Bacc("TRN2", target_bir_lowering=False, num_devices=1)
    B, N, D = x.shape
    E, F2, _ = L0_ffn_gate_up_proj.shape
    F = F2 // 2
    lay = np.ascontiguousarray
    up = np.asarray(L0_ffn_gate_up_proj).reshape(E, F2, D // P, P).transpose(0, 3, 2, 1).reshape(E, P, D // P * F2)
    down = np.asarray(L0_ffn_down_proj).reshape(E, D, 2, F // 2).transpose(0, 3, 2, 1).reshape(E, F // 2, 2 * D)
    arrays = {
        "x": lay(x),
        "ctxT": lay(np.asarray(ctx_512).transpose(0, 2, 1)),
        "W": lay(np.asarray(L0_xattn_W).reshape(2, -1).T),
        "b": lay(np.asarray(L0_xattn_b).reshape(1, 1)),
        "g_xattn": lay(np.asarray(g_xattn).reshape(1, 1)),
        "g_ffn": lay(np.asarray(g_ffn).reshape(1, 1)),
        "gwT": lay(np.asarray(L0_ffn_gate_weight).T),
        "wupT": lay(up),
        "wdnT": lay(down),
        "sim": lay(L0_ffn_similarity),
    }
    args = [nc.dram_tensor(k, list(a.shape), mybir.dt.from_np(a.dtype), kind="ExternalInput").ap()
            for k, a in arrays.items()]
    out = nc.dram_tensor("out", [B * N + P, D], F32, kind="ExternalOutput").ap()
    build(nc, *args, out)
    r = run_bass_kernel_spmd(nc, [arrays], core_ids=[0])
    return r.results[0]["out"][:B * N].reshape(B, N, D)
```
